# Optimizing a Trainium2 kernel written in Bass

```python
import numpy as np
import jax
import jax.numpy as jnp

def _softmax(x, axis=-1):
    return jax.nn.softmax(x, axis=axis)

def _gelu(x):
    return jax.nn.gelu(x, approximate=True)

def _silu(x):
    return jax.nn.silu(x)

def _sigmoid(x):
    return jax.nn.sigmoid(x)

def _layernorm(x, axis=-1, eps=1e-05):
    m = jnp.mean(x, axis=axis, keepdims=True)
    v = jnp.var(x, axis=axis, keepdims=True)
    return (x - m) / jnp.sqrt(v + eps)

def _scatter_add(tgt, idx, src, axis=0):
    return tgt.at[idx].add(src)

def _segment_sum(src, seg, n):
    return jax.ops.segment_sum(src, seg, n)
kernel_name = 'mk_xattn_ffn_d1_seqx_r4_5a819e'

def setup_inputs(seed: int=0):
    np.random.seed(seed)
    _w = jnp.asarray

    def _rec_inputs():
        import jax
        import jax.numpy as jnp
        _rk = jax.random.key(seed)
        x = -0.0003542 + 1 * jax.random.normal(jax.random.fold_in(_rk, 1), (128, 128, 256), jnp.float32)
        _lenS = 128 - jax.random.randint(jax.random.fold_in(_rk, 7), (128,), 0, max(1, 128 // 4) + 1, jnp.int32)
        _lenS2 = 128 - jax.random.randint(jax.random.fold_in(_rk, 8), (128,), 0, max(1, 128 // 4) + 1, jnp.int32)
        _ctx_1024P = jax.random.normal(jax.random.fold_in(_rk, 11), (128, 16, 256), jnp.float32)
        _ctx_1024c = jax.random.dirichlet(jax.random.fold_in(_rk, 511), 0.3 * jnp.ones((16,), jnp.float32), (128, 128))
        _ctx_1024t = jnp.einsum('bsk,bkd->bsd', _ctx_1024c, _ctx_1024P)
        _ctx_1024t = _ctx_1024t * jax.lax.rsqrt(jnp.mean(jnp.square(_ctx_1024t)) + 1e-12) * 0.953939
        ctx_1024 = -4.4511e-05 + 0.999885 * (_ctx_1024t + 0.3 * jax.random.normal(jax.random.fold_in(_rk, 611), (128, 128, 256), jnp.float32))
        return (x, ctx_1024)
    x, ctx_1024 = _rec_inputs()

    def _L0_xattn_setup():
        import jax, jax.numpy as jnp
        import numpy as np
        D_MODEL = 256
        NUM_HEADS = 16
        MAX_LEN = 125
        D_K = D_MODEL // NUM_HEADS
        key = jax.random.key(seed)
        ks = jax.random.split(key, 10)
        B, L = (8, 125)
        s = 1.0 / np.sqrt(D_MODEL)
        return {'query': jax.random.normal(ks[0], (B, L, D_MODEL), dtype=jnp.float32), 'key': jax.random.normal(ks[1], (B, L, D_MODEL), dtype=jnp.float32), 'value': jax.random.normal(ks[2], (B, L, D_MODEL), dtype=jnp.float32), 'Wq': jax.random.normal(ks[3], (D_MODEL, D_MODEL), dtype=jnp.float32) * s, 'bq': jnp.zeros((D_MODEL,), dtype=jnp.float32), 'Wk': jax.random.normal(ks[4], (D_MODEL, D_MODEL), dtype=jnp.float32) * s, 'bk': jnp.zeros((D_MODEL,), dtype=jnp.float32), 'Wv': jax.random.normal(ks[5], (D_MODEL, D_MODEL), dtype=jnp.float32) * s, 'bv': jnp.zeros((D_MODEL,), dtype=jnp.float32), 'rel_emb': jax.random.normal(ks[6], (NUM_HEADS, 2 * MAX_LEN - 1), dtype=jnp.float32)}
    _L0_xattn_all = _L0_xattn_setup()
    _L0_xattn_in = {k: v for k, v in _L0_xattn_all.items() if k in ('Wq', 'bq', 'Wk', 'bk', 'Wv', 'bv', 'rel_emb')}
    del _L0_xattn_all

    def _L0_ffn_setup():
        import jax, jax.numpy as jnp
        import numpy as np
        B, S, D = (4, 1024, 256)
        E, F_EXP = (16, 512)
        F_C = 2.0
        F_SH = 512
        key = jax.random.key(seed)
        ks = jax.random.split(key, 8)
        s = 0.02
        return {'hidden_states': jax.random.normal(ks[0], (B, S, D), jnp.float32), 'gate_w': jax.random.normal(ks[1], (E, D), jnp.float32) * s, 'Wg': jax.random.normal(ks[2], (E, F_EXP, D), jnp.float32) * s, 'Wu': jax.random.normal(ks[3], (E, F_EXP, D), jnp.float32) * s, 'Wd': jax.random.normal(ks[4], (E, D, F_EXP), jnp.float32) * s, 'Ws_g': jax.random.normal(ks[5], (F_SH, D), jnp.float32) * s, 'Ws_u': jax.random.normal(ks[6], (F_SH, D), jnp.float32) * s, 'Ws_d': jax.random.normal(ks[7], (D, F_SH), jnp.float32) * s}
    _L0_ffn_all = _L0_ffn_setup()
    _L0_ffn_in = {k: v for k, v in _L0_ffn_all.items() if k in ('gate_w', 'Wg', 'Wu', 'Wd', 'Ws_g', 'Ws_u', 'Ws_d')}
    del _L0_ffn_all
    return {'x': x, 'ctx_1024': ctx_1024, 'L0_xattn_Wq': _L0_xattn_in['Wq'], 'L0_xattn_bq': _L0_xattn_in['bq'], 'L0_xattn_Wk': _L0_xattn_in['Wk'], 'L0_xattn_bk': _L0_xattn_in['bk'], 'L0_xattn_Wv': _L0_xattn_in['Wv'], 'L0_xattn_bv': _L0_xattn_in['bv'], 'L0_xattn_rel_emb': _L0_xattn_in['rel_emb'], 'L0_ffn_gate_w': _L0_ffn_in['gate_w'], 'L0_ffn_Wg': _L0_ffn_in['Wg'], 'L0_ffn_Wu': _L0_ffn_in['Wu'], 'L0_ffn_Wd': _L0_ffn_in['Wd'], 'L0_ffn_Ws_g': _L0_ffn_in['Ws_g'], 'L0_ffn_Ws_u': _L0_ffn_in['Ws_u'], 'L0_ffn_Ws_d': _L0_ffn_in['Ws_d']}

def reference(x, ctx_1024, L0_xattn_Wq, L0_xattn_bq, L0_xattn_Wk, L0_xattn_bk, L0_xattn_Wv, L0_xattn_bv, L0_xattn_rel_emb, L0_ffn_gate_w, L0_ffn_Wg, L0_ffn_Wu, L0_ffn_Wd, L0_ffn_Ws_g, L0_ffn_Ws_u, L0_ffn_Ws_d):
    import jax
    import jax.numpy as jnp

    def _L0_xattn_ref(query, key, value, Wq, bq, Wk, bk, Wv, bv, rel_emb):
        import jax, jax.numpy as jnp
        import numpy as np
        D_MODEL = 256
        NUM_HEADS = 16
        MAX_LEN = 125
        D_K = D_MODEL // NUM_HEADS
        B, Lq, _ = query.shape
        Lk = key.shape[1]
        H, dk = (NUM_HEADS, D_K)
        q = (query @ Wq + bq).reshape(B, Lq, H, dk).transpose(0, 2, 1, 3)
        k = (key @ Wk + bk).reshape(B, Lk, H, dk).transpose(0, 2, 1, 3)
        v = (value @ Wv + bv).reshape(B, Lk, H, dk).transpose(0, 2, 1, 3)
        scores = jnp.einsum('bhqd,bhkd->bhqk', q, k) / jnp.sqrt(jnp.float32(dk))
        rel_idx = jnp.arange(Lq)[:, None] - jnp.arange(Lk)[None, :] + MAX_LEN - 1
        bias = rel_emb[:, rel_idx]
        scores = scores + bias[None]
        attn = jax.nn.softmax(scores, axis=-1)
        out = jnp.einsum('bhqk,bhkd->bhqd', attn, v)
        return out.transpose(0, 2, 1, 3).reshape(B, Lq, H * dk)

    def _L0_ffn_ref(hidden_states, gate_w, Wg, Wu, Wd, Ws_g, Ws_u, Ws_d):
        import jax, jax.numpy as jnp
        import numpy as np
        B, S, D = (4, 1024, 256)
        E, F_EXP = (16, 512)
        F_C = 2.0
        F_SH = 512
        b, s, d = hidden_states.shape
        e = gate_w.shape[0]
        cap = int(s * F_C / e)
        logits = jnp.einsum('bsd,ed->bse', hidden_states, gate_w)
        scores = jax.nn.softmax(logits, axis=-1).transpose(0, 2, 1)
        topk_w, topk_idx = jax.lax.top_k(scores, cap)
        x_tok = jnp.take_along_axis(hidden_states[:, None, :, :], topk_idx[..., None], axis=2)
        g = jnp.einsum('becd,efd->becf', x_tok, Wg)
        u = jnp.einsum('becd,efd->becf', x_tok, Wu)
        h = jax.nn.gelu(g, approximate=False) * u
        eo = jnp.einsum('becf,edf->becd', h, Wd) * topk_w[..., None]
        offs = (jnp.arange(b) * s)[:, None, None]
        flat_idx = (topk_idx + offs).reshape(-1)
        flat = jnp.zeros((b * s, d), hidden_states.dtype)
        flat = flat.at[flat_idx].add(eo.reshape(-1, d))
        out = flat.reshape(b, s, d)
        gs = jnp.einsum('bsd,fd->bsf', hidden_states, Ws_g)
        us = jnp.einsum('bsd,fd->bsf', hidden_states, Ws_u)
        shared = jnp.einsum('bsf,df->bsd', jax.nn.gelu(gs, approximate=False) * us, Ws_d)
        return out + shared
    x = x + _L0_xattn_ref(_layernorm(x, axis=-1), ctx_1024, ctx_1024, L0_xattn_Wq, L0_xattn_bq, L0_xattn_Wk, L0_xattn_bk, L0_xattn_Wv, L0_xattn_bv, L0_xattn_rel_emb)
    x = x + _L0_ffn_ref(_layernorm(x, axis=-1), L0_ffn_gate_w, L0_ffn_Wg, L0_ffn_Wu, L0_ffn_Wd, L0_ffn_Ws_g, L0_ffn_Ws_u, L0_ffn_Ws_d)
    return x

_drawn_inputs = setup_inputs


def setup_inputs(seed=0):
    import zlib

    import numpy as np

    out = dict(_drawn_inputs(seed))
    spreads = {'L0_xattn_bq': (0.0, 0.359), 'L0_xattn_bk': (0.0, 2.0), 'L0_xattn_bv': (0.0, 0.1)}
    factors = {'L0_ffn_gate_w': 8.0,
     'L0_ffn_Wg': 8.0,
     'L0_ffn_Wu': 8.0,
     'L0_ffn_Wd': 8.0,
     'L0_ffn_Ws_g': 8.0,
     'L0_ffn_Ws_u': 8.0,
     'L0_ffn_Ws_d': 8.0}
    for name, (base, spread) in spreads.items():
        noise = np.random.default_rng([zlib.crc32(name.encode()), seed]).standard_normal(out[name].shape)
        drawn = base * np.exp(spread * noise) if base else spread * noise
        out[name] = jnp.asarray(drawn.astype(out[name].dtype))
    for name, factor in factors.items():
        out[name] = (out[name] * factor).astype(out[name].dtype)
    return out
```

```python
import concourse.bass as bass
from concourse import mybir
from contextlib import ExitStack

B, S, D = 128, 128, 256
H = 16
DK = D // H
E = 16
F = 512
CAP = S * 2 // E
P = 128
DC = D // P
FC = F // P
G = 4
GH = H // G
VW = DK + 1
EPS = 1e-5
LOWEST = -3.0e38
MAXLEN = 125
RELS = 2 * S - 1

fp32 = mybir.dt.float32
f32r = mybir.dt.float32r
u32 = mybir.dt.uint32
ALU = mybir.AluOpType
ACT = mybir.ActivationFunctionType
AX = mybir.AxisListType


def head_of(group, j):
    return (j // 2) * (H // 2) + 2 * group + j % 2


def wait(eng, sem, n):
    if not (isinstance(n, int) and n <= 0):
        eng.wait_ge(sem, n)


def count(eng, n):
    if not isinstance(n, int):
        eng.compute_val(n)
    return n


def batches(eng, body):
    for b in range(4):
        body(b, b % 2)
    with eng.Fori(2, B // 2 - 1) as i:
        for s in range(2):
            body(2 * i + s, s)
    for b in range(B - 2, B):
        body(b, b % 2)


def at_least(b, n):
    return not isinstance(b, int) or b >= n


def below(b, n):
    return not isinstance(b, int) or b < n


def attention_phase(nc, sem, x, ctx_in, wq, wk, wv, bq, bk, bv, rel, gate, x1_d, xn_d, lg_d):
    with ExitStack() as ctx:
        def sb(name, shape, dt=fp32):
            return ctx.enter_context(nc.sbuf_tensor(name, shape, dt))

        def pb(name, shape):
            return ctx.enter_context(nc.psum_tensor(name, shape, fp32))

        ident = sb("a_ident", [P, P])
        flip = sb("flip", [P, P])
        wq_s = sb("wq_s", [P, DC, D])
        wk_s = sb("wk_s", [P, DC, D])
        wv_s = sb("wv_s", [P, DC, D])
        gate_s = sb("gate_s", [P, DC, E])
        bq_s = sb("bq_s", [P, DC])
        bk_s = sb("bk_s", [P, DC])
        bv_row = sb("bv_row", [1, D])
        bv_all = sb("bv_all", [P, D])
        bias_in = sb("bias_in", [P, H, S])
        nbias = sb("nbias", [P, G, GH, S])
        parity = sb("parity", [P, 2])
        ppow = sb("ppow", [P, 1])
        epsc = sb("epsc", [P, 1])
        xt = [sb(f"xt{s}", [P, D]) for s in range(2)]
        ct = [sb(f"ct{s}", [P, D]) for s in range(2)]
        xb = [sb(f"xb{s}", [P, D]) for s in range(2)]
        xn = [sb(f"xn{s}", [P, D]) for s in range(2)]
        st1 = [sb(f"st1{s}", [P, 6]) for s in range(2)]
        mv1 = [sb(f"mv1{s}", [P, 2]) for s in range(2)]
        rs1 = [sb(f"rs1{s}", [P, 2]) for s in range(2)]
        xcT = [sb(f"xcT{s}", [P, 4, P]) for s in range(2)]
        qm = [sb(f"qm{s}", [P, DC, 2, P]) for s in range(2)]
        kT = [sb(f"kT{s}", [P, DC, P]) for s in range(2)]
        v1 = [sb(f"v1{s}", [P, H, VW]) for s in range(2)]
        sc = [sb(f"sc{s}", [P, G, GH, S]) for s in range(2)]
        nmax = [sb(f"nmax{s}", [P, G, GH]) for s in range(2)]
        pr = [sb(f"pr{s}", [P, G, GH, S]) for s in range(2)]
        pT = [sb(f"pT{s}", [P, G, GH, S]) for s in range(2)]
        rinv = [sb(f"rinv{s}", [P, H]) for s in range(2)]
        att = [sb(f"att{s}", [P, D]) for s in range(2)]
        x1 = [sb(f"x1{s}", [P, D]) for s in range(2)]
        st2 = [sb(f"st2{s}", [P, 6]) for s in range(2)]
        mv2 = [sb(f"mv2{s}", [P, 2]) for s in range(2)]
        rs2 = [sb(f"rs2{s}", [P, 2]) for s in range(2)]
        x2 = [sb(f"x2{s}", [P, D]) for s in range(2)]
        x2T = [sb(f"x2T{s}", [P, DC, P]) for s in range(2)]
        lg = [sb(f"lg{s}", [E, S]) for s in range(2)]

        s_ps = [pb(f"s_ps{g}", [P, GH, S]) for g in range(G)]
        front = pb("front", [P, 4, P])
        ring = [pb("ringA", [P, 4, P]), pb("ringB", [P, 4, P])]
        o_ps = pb("o_ps", [P, H, VW])

        const_ld = sem("const_ld")
        ident0 = sem("ident0")
        par0 = sem("par0")
        flip_made = sem("flip_made")
        flipped = sem("flipped")
        const_pool = sem("const_pool")
        const_dve = sem("const_dve")
        x_ld = [sem(f"x_ld{s}") for s in range(2)]
        c_ld = [sem(f"c_ld{s}") for s in range(2)]
        xb_done = sem("xb_done")
        stats1 = sem("stats1")
        var1 = sem("var1")
        eps1 = sem("eps1")
        rstd1 = sem("rstd1")
        xn_done = sem("xn_done")
        t_done = sem("t_done")
        xcT_done = sem("xcT_done")
        qk_done = sem("qk_done")
        v_done = sem("v_done")
        q_done = sem("q_done")
        kT_done = sem("kT_done")
        v1_done = sem("v1_done")
        s_done = sem("s_done")
        max_done = sem("max_done")
        exp_done = sem("exp_done")
        pt_done = sem("pt_done")
        pT_done = sem("pT_done")
        av_done = sem("av_done")
        rinv_done = sem("rinv_done")
        att_done = sem("att_done")
        x1_done = sem("x1_done")
        stats2 = sem("stats2")
        var2 = sem("var2")
        eps2 = sem("eps2")
        rstd2 = sem("rstd2")
        x2_done = sem("x2_done")
        x2t_done = sem("x2t_done")
        x2T_done = sem("x2T_done")
        lgp_done = sem("lgp_done")
        lg_done = sem("lg_done")
        x1_st = [sem(f"x1_st{s}") for s in range(2)]
        x2_st = [sem(f"x2_st{s}") for s in range(2)]
        lg_st = [sem(f"lg_st{s}") for s in range(2)]

        def rounds(b, s):
            return b // 2 + 1 if isinstance(b, int) else (b - s) // 2 + 1

        block = ctx.enter_context(nc.Block())

        @block.sync
        def _(sp):
            n_const = 0
            for dst, src in ((wq_s, wq), (wk_s, wk), (wv_s, wv)):
                sp.dma_start(dst[:, :, :], src.rearrange("(c p) n -> p c n", p=P)).then_inc(const_ld, 16)
            sp.dma_start(gate_s[:, :, :], gate.rearrange("(c p) n -> p c n", p=P)).then_inc(const_ld, 16)
            with nc.allow_non_contiguous_dma(reason="a bias vector is spread over the partitions once"):
                sp.dma_start(bq_s[:, :], bq.rearrange("(c p) -> p c", p=P)).then_inc(const_ld, 16)
                sp.dma_start(bk_s[:, :], bk.rearrange("(c p) -> p c", p=P)).then_inc(const_ld, 16)
            sp.dma_start(bv_row[:, :], bv.rearrange("(a n) -> a n", a=1)).then_inc(const_ld, 16)
            for h in range(H):
                win = bass.AP(rel.tensor, h * RELS, [[1, P], [1, S]])
                sp.dma_start(bias_in[:, h, :], win).then_inc(const_ld, 16)

            def load_x(b, s):
                wait(sp, xn_done, b - 1)
                wait(sp, xb_done, b - 1)
                sp.dma_start(xt[s][:, :], x[b]).then_inc(x_ld[s], 16)

            def load_ctx(b, s):
                wait(sp, t_done, b - 1)
                sp.dma_start(ct[s][:, :], ctx_in[b]).then_inc(c_ld[s], 16)

            load_x(0, 0)
            load_ctx(0, 0)
            load_x(1, 1)
            load_ctx(1, 1)
            load_x(2, 0)

            def store_rows(b, s):
                sp.wait_ge(x1_done, b + 1)
                sp.dma_start(x1_d[b], x1[s][:, :]).then_inc(x1_st[s], 16)
                sp.wait_ge(x2_done, b + 1)
                sp.dma_start(xn_d[b], x2[s][:, :]).then_inc(x2_st[s], 16)

            def store_logits(b, s):
                sp.wait_ge(lg_done, b + 1)
                sp.dma_start(lg_d[b], lg[s][:, :]).then_inc(lg_st[s], 16)

            def body(b, s):
                if below(b, B - 3):
                    load_x(b + 3, 1 - s)
                if below(b, B - 2):
                    load_ctx(b + 2, s)
                if at_least(b, 1):
                    store_rows(b - 1, 1 - s)
                if at_least(b, 2):
                    store_logits(b - 2, s)

            for b in range(4):
                body(b, b % 2)
            with sp.Fori(2, B // 2 - 2) as i:
                for s in range(2):
                    body(2 * i + s, s)
            for b in range(B - 4, B):
                body(b, b % 2)
            store_rows(B - 1, 1)
            store_logits(B - 2, 0)
            store_logits(B - 1, 1)
            for s in range(2):
                for done in (x1_st[s], x2_st[s], lg_st[s]):
                    sp.wait_ge(done, 16 * B // 2)

        @block.gpsimd
        def _(pool):
            pool.memset(ident[:, :], 0.0).then_inc(ident0, 1)
            pool.memset(flip[:, :], 0.0).then_inc(ident0, 1)
            pool.memset(parity[:, :], 0.0).then_inc(par0, 1)
            pool.memset(ppow[:, :], -0.5)
            pool.memset(epsc[:, :], EPS)
            pool.wait_ge(ident0, 2)
            pool.affine_select(out=flip[:, :], in_=flip[:, :], compare_op=ALU.not_equal, fill=-1.0,
                               base=1 - P, pattern=[[1, P]], channel_multiplier=1).then_inc(flip_made, 1)
            pool.affine_select(out=ident[:, :], in_=ident[:, :], compare_op=ALU.not_equal, fill=1.0,
                               base=0, pattern=[[-1, P]], channel_multiplier=1).then_inc(const_pool, 1)
            pool.wait_ge(const_ld, 16 * (7 + H))
            pool.partition_broadcast(bv_all[:, :], bv_row[0:1, :], channels=P).then_inc(const_pool, 1)
            pool.wait_ge(const_pool, 2)

            def keep_residual(b, s):
                pool.wait_ge(x_ld[s], 16 * rounds(b, s))
                wait(pool, x1_done, b - 1)
                pool.tensor_tensor(xb[s][:, :], xt[s][:, :], bv_all[:, :], ALU.add).then_inc(xb_done, 1)

            def inverse_root(b, s, stats, mv, rs, eps, rstd):
                pool.wait_ge(stats, b + 1)
                pool.tensor_tensor(rs[s][:, 1:2], mv[s][:, 1:2], epsc[:, :], ALU.add).then_inc(eps, 1)
                pool.wait_ge(eps, b + 1)
                pool.tensor_tensor(rs[s][:, 0:1], rs[s][:, 1:2], ppow[:, :], ALU.pow).then_inc(rstd, 1)

            keep_residual(0, 0)
            inverse_root(0, 0, stats1, mv1, rs1, eps1, rstd1)
            keep_residual(1, 1)
            inverse_root(1, 1, stats1, mv1, rs1, eps1, rstd1)

            def second_norm(b, s):
                inverse_root(b, s, stats2, mv2, rs2, eps2, rstd2)
                ready, used, stored = count(pool, b + 1), count(pool, b - 1), count(pool, 16 * (rounds(b, s) - 1))
                pool.wait_ge(const_pool, 2)
                pool.wait_ge(rstd2, ready)
                wait(pool, x2t_done, used)
                wait(pool, x2_st[s], stored)
                pool.tensor_scalar(x2[s][:, :], x1[s][:, :], mv2[s][:, 0:1], rs2[s][:, 0:1],
                                   ALU.subtract, ALU.mult).then_inc(x2_done, 1)

            def body(b, s):
                if at_least(b, 1):
                    second_norm(b - 1, 1 - s)
                if below(b, B - 2):
                    inverse_root(b + 2, s, stats1, mv1, rs1, eps1, rstd1)
                pool.wait_ge(att_done, b + 1)
                if at_least(b, 2):
                    pool.wait_ge(x1_st[s], 16 * (rounds(b, s) - 1))
                pool.tensor_tensor(x1[s][:, :], att[s][:, :], xb[s][:, :], ALU.add).then_inc(x1_done, 1)
                if below(b, B - 2):
                    keep_residual(b + 2, s)

            batches(pool, body)
            second_norm(B - 1, 1)

        @block.tensor
        def _(pe):
            pe.wait_ge(const_ld, 16 * (7 + H))
            pe.wait_ge(const_pool, 1)
            pe.wait_ge(flip_made, 1)
            for g in range(G):
                for j in range(GH):
                    last = pe.matmul(s_ps[g][:, j, :], flip[:, :], bias_in[:, head_of(g, j), :], start=True, stop=True)
            last.then_inc(flipped, 1)

            def transposes(b, s):
                pe.wait_ge(xn_done, b + 1)
                pe.wait_ge(c_ld[s], 16 * rounds(b, s))
                wait(pe, q_done, 4 * b)
                wait(pe, kT_done, b)
                for c in range(DC):
                    pe.transpose(front[:, c, :], xn[s][:, c * P:(c + 1) * P], ident[:, :])
                for c in range(DC):
                    last = pe.transpose(front[:, DC + c, :], ct[s][:, c * P:(c + 1) * P], ident[:, :])
                last.then_inc(t_done, 1)

            def project_qk(b, s):
                pe.wait_ge(xcT_done, b + 1)
                for w, o in ((wq_s, 0), (wk_s, DC)):
                    for m in range(DC):
                        for c in range(DC):
                            last = pe.matmul(front[:, o + m, :], w[:, c, m * P:(m + 1) * P], xcT[s][:, o + c, :],
                                             start=c == 0, stop=c == DC - 1)
                last.then_inc(qk_done, 1)

            def project_v(b, s):
                wait(pe, lg_done, b - 2)
                wait(pe, pT_done, 4 * b - 5)
                out = ring[1][:, 0:2, :].rearrange("p a n -> p (a n)")
                for c in range(DC):
                    last = pe.matmul(out, xcT[s][:, DC + c, :], wv_s[:, c, :], start=c == 0, stop=c == DC - 1)
                last.then_inc(v_done, 1)

            def scores(b, s):
                if isinstance(b, int) and b == 0:
                    pe.wait_ge(const_dve, 6)
                wait(pe, max_done, H * b)
                pe.wait_ge(q_done, 4 * (b + 1))
                pe.wait_ge(kT_done, b + 1)
                for j in range(GH):
                    for g in range(G):
                        rows = slice(32 * g, 32 * g + 32)
                        last = pe.matmul(s_ps[g][:, j, :], qm[s][rows, j // 2, j % 2, :], kT[s][rows, j // 2, :],
                                         start=True, stop=True)
                last.then_inc(s_done, 1)

            def probs_T(b, s, g):
                pe.wait_ge(exp_done, H * b + GH * (g + 1))
                if g == 1:
                    pe.wait_ge(pT_done, 4 * b + 1)
                elif g == 2:
                    if below(b, B - 1):
                        pe.wait_ge(v1_done, b + 2)
                    if at_least(b, 3):
                        pe.wait_ge(x2T_done, b - 2)
                elif g == 3:
                    pe.wait_ge(pT_done, 4 * b + 2)
                else:
                    wait(pe, pT_done, 4 * b)
                bank = ring[1] if g == 2 else ring[0]
                for j in range(GH):
                    last = pe.transpose(bank[:, j, :], pr[s][:, g, j, :], ident[:, :])
                last.then_inc(pt_done, 1)

            def weigh_values(b, s, g):
                pe.wait_ge(pT_done, 4 * b + g + 1)
                if g == 0:
                    pe.wait_ge(v1_done, b + 1)
                    wait(pe, att_done, b)
                for j in range(GH):
                    last = pe.matmul(o_ps[:, head_of(g, j), :], pT[s][:, g, j, :], v1[s][:, head_of(g, j), :],
                                     start=True, stop=True)
                if g == G - 1:
                    last.then_inc(av_done, 1)

            def rows_T(b, s):
                pe.wait_ge(x2_done, b + 1)
                pe.wait_ge(pT_done, 4 * b + 7 if not isinstance(b, int) or b < B - 1 else 4 * B)
                for c in range(DC):
                    last = pe.transpose(ring[1][:, c, :], x2[s][:, c * P:(c + 1) * P], ident[:, :])
                last.then_inc(x2t_done, 1)

            def logits(b, s):
                pe.wait_ge(x2T_done, b + 1)
                for c in range(DC):
                    last = pe.matmul(ring[1][0:E, 2, :], gate_s[:, c, :], x2T[s][:, c, :],
                                     start=c == 0, stop=c == DC - 1)
                last.then_inc(lgp_done, 1)

            transposes(0, 0)
            project_qk(0, 0)
            project_v(0, 0)
            scores(0, 0)

            def body(b, s):
                if below(b, B - 1):
                    transposes(b + 1, 1 - s)
                if at_least(b, 2):
                    logits(b - 2, s)
                probs_T(b, s, 0)
                if below(b, B - 1):
                    project_qk(b + 1, 1 - s)
                    project_v(b + 1, 1 - s)
                probs_T(b, s, 1)
                weigh_values(b, s, 0)
                probs_T(b, s, 2)
                weigh_values(b, s, 1)
                probs_T(b, s, 3)
                if below(b, B - 1):
                    scores(b + 1, 1 - s)
                weigh_values(b, s, 2)
                weigh_values(b, s, 3)
                if at_least(b, 1):
                    rows_T(b - 1, 1 - s)

            batches(pe, body)
            logits(B - 2, 0)
            pe.wait_ge(lg_done, B - 1)
            rows_T(B - 1, 1)
            logits(B - 1, 1)

        @block.scalar
        def _(act):
            def front_T(b, s):
                act.wait_ge(t_done, b + 1)
                wait(act, v_done, b - 1)
                act.activation(xcT[s][:, :, :], front[:, :, :], ACT.Copy).then_inc(xcT_done, 1)

            def keys(b, s):
                act.wait_ge(q_done, 4 * (b + 1))
                wait(act, s_done, b - 1)
                for c in range(DC):
                    last = act.activation(kT[s][:, c, :], front[:, DC + c, :], ACT.Identity, bias=bk_s[:, c:c + 1])
                last.then_inc(kT_done, 1)

            def values(b, s):
                act.wait_ge(v_done, b + 1)
                wait(act, av_done, b - 1)
                act.activation(v1[s][:, :, 0:DK],
                               ring[1][:, 0:2, :].rearrange("p a (h d) -> p (a h) d", d=DK),
                               ACT.Copy).then_inc(v1_done, 1)

            def exps(b, s, g):
                wait(act, pt_done, 4 * (b - 2) + g + 1)
                for j in range(GH):
                    act.wait_ge(max_done, H * b + GH * g + j + 1)
                    act.activation(pr[s][:, g, j, :], sc[s][:, g, j, :], ACT.Exp,
                                   bias=nmax[s][:, g, j:j + 1], scale=-1.0).then_inc(exp_done, 1)

            def rows(b, s):
                act.wait_ge(x2t_done, b + 1)
                wait(act, lgp_done, b - 1)
                act.activation(x2T[s][:, :, :], ring[1][:, 0:DC, :], ACT.Copy).then_inc(x2T_done, 1)

            def logits(b, s):
                act.wait_ge(lgp_done, b + 1)
                if at_least(b, 2):
                    act.wait_ge(lg_st[s], 16 * (rounds(b, s) - 1))
                act.activation(lg[s][:, :], ring[1][0:E, 2, :], ACT.Copy).then_inc(lg_done, 1)

            front_T(0, 0)
            act.wait_ge(const_ld, 16 * (7 + H))
            keys(0, 0)
            act.wait_ge(const_dve, 3)
            values(0, 0)

            def body(b, s):
                if below(b, B - 1):
                    front_T(b + 1, 1 - s)
                if at_least(b, 2):
                    logits(b - 2, s)
                exps(b, s, 0)
                if below(b, B - 1):
                    keys(b + 1, 1 - s)
                exps(b, s, 1)
                if below(b, B - 1):
                    values(b + 1, 1 - s)
                exps(b, s, 2)
                exps(b, s, 3)
                if at_least(b, 1):
                    rows(b - 1, 1 - s)

            batches(act, body)
            logits(B - 2, 0)
            rows(B - 1, 1)
            logits(B - 1, 1)

        @block.vector
        def _(dve):
            for s in range(2):
                dve.memset(v1[s][:, :, DK:VW], 1.0).then_inc(const_dve, 1)
            dve.wait_ge(const_pool, 2)
            dve.wait_ge(par0, 1)
            blocks = ident[:, :].rearrange("p (a j d) -> p j a d", j=2, d=DK)
            for j in range(2):
                dve.tensor_reduce(parity[:, j:j + 1], blocks[:, j, :, :], AX.XY, ALU.add).then_inc(const_dve, 1)
            dve.wait_ge(const_dve, 4)
            dve.tensor_scalar(parity[:, :], parity[:, :], -float(DK) ** -0.5, None, ALU.mult).then_inc(const_dve, 1)
            dve.wait_ge(const_ld, 16 * (7 + H))
            dve.wait_ge(flipped, 1)
            for g in range(G):
                last = dve.tensor_copy(nbias[:, g, :, :], s_ps[g][:, :, :])
            last.then_inc(const_dve, 1)
            dve.wait_ge(const_dve, 6)

            def stats(src, b, s, st, mv, var, done):
                dve.bn_stats(st[s][:, :], src[s][:, :]).then_inc(var, 1)
                ready = count(dve, b + 1)
                dve.wait_ge(const_dve, 6)
                dve.wait_ge(var, ready)
                dve.bn_aggr(mv[s][:, :], st[s][:, :]).then_inc(done, 1)

            def stats_in(b, s):
                dve.wait_ge(x_ld[s], 16 * rounds(b, s))
                wait(dve, rstd1, b - 1)
                stats(xt, b, s, st1, mv1, var1, stats1)

            def norm_in(b, s):
                dve.wait_ge(rstd1, b + 1)
                wait(dve, t_done, b - 1)
                dve.tensor_scalar(xn[s][:, :], xt[s][:, :], mv1[s][:, 0:1], rs1[s][:, 0:1],
                                  ALU.subtract, ALU.mult).then_inc(xn_done, 1)

            def queries(b, s):
                dve.wait_ge(qk_done, b + 1)
                wait(dve, s_done, b - 1)
                for c in range(DC):
                    for j in range(2):
                        dve.tensor_scalar(qm[s][:, c, j, :], front[:, c, :], bq_s[:, c:c + 1], parity[:, j:j + 1],
                                          ALU.add, ALU.mult).then_inc(q_done, 1)

            def add_bias_and_max(b, s, g):
                ready, used = count(dve, b + 1), count(dve, H * (b - 2) + GH * (g + 1))
                dve.wait_ge(const_dve, 6)
                if g == 0:
                    dve.wait_ge(s_done, ready)
                wait(dve, exp_done, used)
                for j in range(GH):
                    dve.tensor_tensor_reduce(out=sc[s][:, g, j, :], in0=s_ps[g][:, j, :], in1=nbias[:, g, j, :],
                                             scale=1.0, scalar=-LOWEST, op0=ALU.add, op1=ALU.min,
                                             accum_out=nmax[s][:, g, j:j + 1]).then_inc(max_done, 1)

            def probs_out(b, s, g):
                dve.wait_ge(pt_done, 4 * b + g + 1)
                if g == 0:
                    wait(dve, av_done, b - 1)
                bank = ring[1] if g == 2 else ring[0]
                dve.tensor_copy(pT[s][:, g, :, :], bank[:, :, :]).then_inc(pT_done, 1)

            def normalise(b, s):
                dve.wait_ge(av_done, b + 1)
                wait(dve, x1_done, b - 1)
                dve.reciprocal(rinv[s][:, :], o_ps[:, :, DK]).then_inc(rinv_done, 1)
                dve.wait_ge(rinv_done, b + 1)
                dve.tensor_tensor(att[s][:, :].rearrange("p (h d) -> p h d", d=DK), o_ps[:, :, 0:DK],
                                  rinv[s][:, :].rearrange("p (h o) -> p h o", o=1).to_broadcast([P, H, DK]),
                                  ALU.mult).then_inc(att_done, 1)

            def stats_out(b, s):
                dve.wait_ge(x1_done, b + 1)
                wait(dve, x2_done, b - 1)
                stats(x1, b, s, st2, mv2, var2, stats2)

            for b in range(2):
                stats_in(b, b)
                norm_in(b, b)
            queries(0, 0)

            def body(b, s):
                add_bias_and_max(b, s, 0)
                if at_least(b, 1):
                    stats_out(b - 1, 1 - s)
                add_bias_and_max(b, s, 1)
                add_bias_and_max(b, s, 2)
                probs_out(b, s, 0)
                add_bias_and_max(b, s, 3)
                if below(b, B - 1):
                    queries(b + 1, 1 - s)
                probs_out(b, s, 1)
                if below(b, B - 2):
                    stats_in(b + 2, s)
                probs_out(b, s, 2)
                if below(b, B - 2):
                    norm_in(b + 2, s)
                probs_out(b, s, 3)
                normalise(b, s)

            batches(dve, body)
            stats_out(B - 1, 1)


def routing_phase(nc, sem, lg_d, gidx, wts, idx_col):
    HALF = E * CAP // P
    with ExitStack() as ctx:
        def sb(name, shape, dt=fp32):
            return ctx.enter_context(nc.sbuf_tensor(name, shape, dt))

        ident = sb("r_ident", [P, P])
        raw = sb("r_raw", [P, E, S])
        ex = sb("r_exp", [P, E, S])
        score = sb("r_score", [P, E, S])
        rest = sb("r_rest", [P, E, S])
        top = sb("r_max", [P, S])
        tot = sb("r_sum", [P, S])
        inv = sb("r_inv", [P, S])
        place = sb("r_place", [P, E, CAP], u32)
        place_f = sb("r_place_f", [P, E * CAP])
        first_row = sb("r_first_row", [P, 1], u32)
        first_row_f = sb("r_first_row_f", [P, 1])
        idx_ps = ctx.enter_context(nc.psum_tensor("r_idx_ps", [P, HALF, P], fp32))

        lg_ld = sem("r_lg_ld")
        zeroed = sem("r_zeroed")
        ident_made = sem("r_ident_made")
        rows_made = sem("r_rows_made")
        step = sem("r_step")
        exp_done = sem("r_exp_done")
        places = sem("r_places")
        turned = sem("r_turned")
        block = ctx.enter_context(nc.Block())

        @block.sync
        def _(sp):
            sp.dma_start(raw[:, :, :], lg_d[:, :, :]).then_inc(lg_ld, 16)

        @block.gpsimd
        def _(pool):
            pool.memset(ident[:, :], 0.0).then_inc(zeroed, 1)
            pool.iota(first_row[:, :], pattern=[[0, 1]], base=0, channel_multiplier=S).then_inc(rows_made, 1)
            pool.wait_ge(zeroed, 1)
            pool.affine_select(out=ident[:, :], in_=ident[:, :], compare_op=ALU.not_equal, fill=1.0,
                               base=0, pattern=[[-1, P]], channel_multiplier=1).then_inc(ident_made, 1)

        @block.scalar
        def _(act):
            act.wait_ge(step, 2)
            act.activation(ex[:, :, :], rest[:, :, :], ACT.Exp).then_inc(exp_done, 1)

        @block.tensor
        def _(pe):
            pe.wait_ge(ident_made, 1)
            pe.wait_ge(places, 1)
            for half in range(HALF):
                last = pe.transpose(idx_ps[:, half, :], place_f[:, half * P:(half + 1) * P], ident[:, :])
            last.then_inc(turned, 1)

        @block.vector
        def _(dve):
            def over_experts(t):
                return t[:, :, :].rearrange("p e t -> p t e")

            def per_token(t):
                return t[:, :].rearrange("p (o t) -> p o t", o=1).to_broadcast([P, E, S])

            dve.wait_ge(lg_ld, 16)
            dve.tensor_reduce(top[:, :], over_experts(raw), AX.X, ALU.max).then_inc(step, 1)
            dve.wait_ge(step, 1)
            dve.tensor_tensor(rest[:, :, :], raw[:, :, :], per_token(top), ALU.subtract).then_inc(step, 1)
            dve.wait_ge(exp_done, 1)
            dve.tensor_reduce(tot[:, :], over_experts(ex), AX.X, ALU.add).then_inc(step, 1)
            dve.wait_ge(step, 3)
            dve.reciprocal(inv[:, :], tot[:, :]).then_inc(step, 1)
            dve.wait_ge(step, 4)
            dve.tensor_tensor(score[:, :, :], ex[:, :, :], per_token(inv), ALU.mult).then_inc(step, 1)
            dve.wait_ge(step, 5)
            for e in range(E):
                dve.max(wts[:, e, 0:8], score[:, e, :]).then_inc(step, 1)
            dve.wait_ge(step, 5 + E)
            for e in range(E):
                dve.max_index(place[:, e, 0:8], wts[:, e, 0:8], score[:, e, :]).then_inc(step, 1)
            for e in range(E):
                dve.match_replace(rest[:, e, :], wts[:, e, 0:8], score[:, e, :], -1.0).then_inc(step, 1)
            dve.wait_ge(step, 5 + 3 * E)
            for e in range(E):
                dve.max(wts[:, e, 8:16], rest[:, e, :]).then_inc(step, 1)
            dve.wait_ge(step, 5 + 4 * E)
            for e in range(E):
                dve.max_index(place[:, e, 8:16], wts[:, e, 8:16], rest[:, e, :]).then_inc(step, 1)
            dve.wait_ge(rows_made, 1)
            dve.wait_ge(step, 5 + 5 * E)
            dve.tensor_copy(place_f[:, :], place[:, :, :].rearrange("p e r -> p (e r)")).then_inc(places, 1)
            dve.tensor_copy(first_row_f[:, :], first_row[:, :]).then_inc(places, 1)
            dve.wait_ge(places, 2)
            dve.tensor_scalar(gidx[:, :], place_f[:, :], first_row_f[:, :], None, ALU.add)
            dve.wait_ge(turned, 1)
            dve.tensor_copy(idx_col[:, :, :], idx_ps[:, :, :])


def expert_phase(nc, sem, xn_rows, wg, wu, wd, gidx, wts, eo_d):
    Q = 4
    R = CAP // Q
    N = R * P
    with ExitStack() as ctx:
        def sb(name, shape, dt=fp32):
            return ctx.enter_context(nc.sbuf_tensor(name, shape, dt))

        def pb(name, shape):
            return ctx.enter_context(nc.psum_tensor(name, shape, fp32))

        ident = sb("e_ident", [P, P])
        raw = [sb(f"e_raw{k}", [P, DC * F]) for k in range(3)]
        whi = [[sb(f"e_whi{k}{s}", [P, DC * F], f32r) for s in range(2)] for k in range(3)]
        wlo = [[sb(f"e_wlo{k}{s}", [P, DC * F], f32r) for s in range(2)] for k in range(3)]
        idx_e = [sb(f"e_idx{s}", [P, CAP], u32) for s in range(2)]
        w_e = [sb(f"e_w{s}", [P, CAP]) for s in range(2)]
        xg = [sb(f"e_xg{s}", [P, R, D]) for s in range(2)]
        xhi = [sb(f"e_xhi{s}", [P, DC, N], f32r) for s in range(2)]
        xlo = [sb(f"e_xlo{s}", [P, DC, N], f32r) for s in range(2)]
        act_g = [sb(f"e_g{s}", [P, N]) for s in range(2)]
        hid = [sb(f"e_h{s}", [P, N]) for s in range(2)]
        hhi = [sb(f"e_hhi{s}", [P, FC, N], f32r) for s in range(2)]
        hlo = [sb(f"e_hlo{s}", [P, FC, N], f32r) for s in range(2)]
        yo = [sb(f"e_yo{s}", [P, R, D]) for s in range(2)]
        x_ps = pb("e_x_ps", [P, DC, N])
        g_ps = [pb(f"e_g_ps{s}", [P, N]) for s in range(2)]
        u_ps = [pb(f"e_u_ps{s}", [P, N]) for s in range(2)]
        y_ps = pb("e_y_ps", [P, R, D])

        ident0 = sem("e_ident0")
        ident_made = sem("e_ident_made")
        w_ld = [sem(f"e_w_ld{k}") for k in range(3)]
        whi_done = sem("e_whi_done")
        wlo_done = sem("e_wlo_done")
        idx_done = sem("e_idx_done")
        we_done = sem("e_we_done")
        xg_ld = [sem(f"e_xg_ld{s}") for s in range(2)]
        xt_done = sem("e_xt_done")
        xhi_done = sem("e_xhi_done")
        xlo_done = sem("e_xlo_done")
        gu_done = sem("e_gu_done")
        gelu_done = sem("e_gelu_done")
        hid_done = sem("e_hid_done")
        hhi_done = sem("e_hhi_done")
        hlo_done = sem("e_hlo_done")
        y_done = sem("e_y_done")
        ya_done = sem("e_ya_done")
        yb_done = sem("e_yb_done")
        y_st = [sem(f"e_y_st{s}") for s in range(2)]
        block = ctx.enter_context(nc.Block())

        w_src = [wg, wu, wd]

        def steps(eng, body):
            for e in range(2):
                for q in range(Q):
                    body(e, e % 2, q)
            with eng.Fori(1, E // 2 - 1) as i:
                for es in range(2):
                    for q in range(Q):
                        body(2 * i + es, es, q)
            for e in range(E - 2, E):
                for q in range(Q):
                    body(e, e % 2, q)

        def rounds(n, s):
            return n // 2 + 1 if isinstance(n, int) else (n - s) // 2 + 1

        @block.sync
        def _(sp):
            def load_weight(e, k):
                wait(sp, wlo_done, 3 * e + k - 2)
                sp.dma_start(raw[k][:, :].rearrange("p (c n) -> p c n", c=D // P if k < 2 else F // P),
                             w_src[k][e].rearrange("(c p) n -> p c n", p=P)).then_inc(w_ld[k], 16)

            for e in range(2):
                for k in range(3):
                    load_weight(e, k)

            def body(e, es, q):
                n = Q * e + q
                sp.wait_ge(ya_done, n + 1)
                sp.wait_ge(yb_done, n + 1)
                sp.dma_start(eo_d[:, e, q * R:(q + 1) * R, :], yo[q % 2][:, :, :]).then_inc(y_st[q % 2], 16)
                if q > 0 and below(e, E - 2):
                    load_weight(e + 2, q - 1)

            steps(sp, body)
            for s in range(2):
                sp.wait_ge(y_st[s], 16 * E * Q // 2)

        @block.gpsimd
        def _(pool):
            pool.memset(ident[:, :], 0.0).then_inc(ident0, 1)
            pool.wait_ge(ident0, 1)
            pool.affine_select(out=ident[:, :], in_=ident[:, :], compare_op=ALU.not_equal, fill=1.0,
                               base=0, pattern=[[-1, P]], channel_multiplier=1).then_inc(ident_made, 1)

            def indices(e, es):
                if at_least(e, 2):
                    for s in range(2):
                        pool.wait_ge(xg_ld[s], 16 * R * (Q // 2) * (e - 1))
                pool.tensor_copy(idx_e[es][:, :], gidx[:, bass.ds(e * CAP, CAP)]).then_inc(idx_done, 1)

            def gather(n, e, es, q):
                ready, used = count(pool, e + 1), count(pool, n - 1)
                pool.wait_ge(ident_made, 1)
                if q == 0:
                    pool.wait_ge(idx_done, ready)
                wait(pool, xt_done, used)
                for r in range(R):
                    pool.indirect_dma_start(
                        out=xg[q % 2][:, r, :], out_offset=None, in_=xn_rows,
                        in_offset=bass.IndirectOffsetOnAxis(ap=idx_e[es][:, q * R + r:q * R + r + 1], axis=0),
                    ).then_inc(xg_ld[q % 2], 16)

            indices(0, 0)
            gather(0, 0, 0, 0)
            gather(1, 0, 0, 1)

            def body(e, es, q):
                n = Q * e + q
                if q == 1 and below(e, E - 1):
                    indices(e + 1, 1 - es)
                if q < Q - 2:
                    gather(n + 2, e, es, q + 2)
                elif below(e, E - 1):
                    gather(n + 2, e + 1, 1 - es, q + 2 - Q)
                for f in range(FC):
                    ready, used = count(pool, FC * n + f + 1), count(pool, n - 1)
                    pool.wait_ge(hhi_done, ready)
                    if f == 0:
                        wait(pool, y_done, used)
                    pool.tensor_tensor(hlo[q % 2][:, f, :], hid[f % 2][:, :], hhi[q % 2][:, f, :].bitcast(fp32),
                                       ALU.subtract).then_inc(hlo_done, 1)

            steps(pool, body)

        @block.tensor
        def _(pe):
            pe.wait_ge(ident_made, 1)

            def slots_T(n, q):
                pe.wait_ge(xg_ld[q % 2], 16 * R * rounds(n, q % 2))
                wait(pe, xlo_done, n)
                for r in range(R):
                    for c in range(DC):
                        last = pe.transpose(x_ps[:, c, r * P:(r + 1) * P], xg[q % 2][:, r, c * P:(c + 1) * P],
                                            ident[:, :])
                last.then_inc(xt_done, 1)

            def up(n, e, es, q, f):
                if f == 0:
                    pe.wait_ge(xlo_done, n + 1)
                    pe.wait_ge(xhi_done, n + 1)
                    if q == 0:
                        pe.wait_ge(wlo_done, 3 * (e + 1))
                wait(pe, hid_done, FC * n + f - 1)
                for k, bank in ((0, g_ps[f % 2]), (1, u_ps[f % 2])):
                    parts = [(w, x, c) for c in range(DC)
                             for w, x in ((whi, xhi), (whi, xlo), (wlo, xhi))]
                    for m, (w, x, c) in enumerate(parts):
                        last = pe.matmul(bank[:, :], w[k][es][:, c * F + f * P:c * F + (f + 1) * P],
                                         x[q % 2][:, c, :], start=m == 0, stop=m == len(parts) - 1)
                last.then_inc(gu_done, 1)

            def down(n, es, q):
                pe.wait_ge(hlo_done, FC * (n + 1))
                wait(pe, ya_done, n)
                wait(pe, yb_done, n)
                for r in range(R):
                    parts = [(h, w, f) for f in range(FC)
                             for h, w in ((hhi, whi), (hhi, wlo), (hlo, whi))]
                    for m, (h, w, f) in enumerate(parts):
                        last = pe.matmul(y_ps[:, r, :], h[q % 2][:, f, r * P:(r + 1) * P],
                                         w[2][es][:, f * D:(f + 1) * D], start=m == 0, stop=m == len(parts) - 1)
                last.then_inc(y_done, 1)

            slots_T(0, 0)

            def body(e, es, q):
                n = Q * e + q
                up(n, e, es, q, 0)
                if q > 0:
                    down(n - 1, es, q - 1)
                elif at_least(e, 1):
                    down(n - 1, 1 - es, Q - 1)
                up(n, e, es, q, 1)
                if below(e, E - 1) or q < Q - 1:
                    slots_T(n + 1, (q + 1) % Q)
                up(n, e, es, q, 2)
                up(n, e, es, q, 3)

            steps(pe, body)
            down(E * Q - 1, 1, Q - 1)

        @block.scalar
        def _(act):
            def slots_hi(n, q):
                act.wait_ge(xt_done, n + 1)
                wait(act, gu_done, FC * (n - 1))
                act.activation(xhi[q % 2][:, :, :], x_ps[:, :, :], ACT.Copy).then_inc(xhi_done, 1)

            def out_half(n, e, es, q):
                act.wait_ge(y_done, n + 1)
                if at_least(n, 2):
                    act.wait_ge(y_st[q % 2], 16 * (rounds(n, q % 2) - 1))
                act.wait_ge(we_done, e + 1)
                for r in range(R // 2):
                    last = act.activation(yo[q % 2][:, r, :], y_ps[:, r, :], ACT.Copy,
                                          scale=w_e[es][:, q * R + r:q * R + r + 1])
                last.then_inc(ya_done, 1)

            slots_hi(0, 0)

            def hidden(n, q, f):
                act.wait_ge(gu_done, FC * n + f + 1)
                wait(act, hid_done, FC * n + f - 1)
                act.activation(act_g[f % 2][:, :], g_ps[f % 2][:, :], ACT.Gelu).then_inc(gelu_done, 1)

            def hidden_hi(n, q, f):
                act.wait_ge(hid_done, FC * n + f + 1)
                if f == 0:
                    wait(act, y_done, n - 1)
                act.activation(hhi[q % 2][:, f, :], hid[f % 2][:, :], ACT.Copy).then_inc(hhi_done, 1)

            def body(e, es, q):
                n = Q * e + q
                hidden(n, q, 0)
                hidden_hi(n, q, 0)
                if q > 0:
                    out_half(n - 1, e, es, q - 1)
                elif at_least(e, 1):
                    out_half(n - 1, e - 1, 1 - es, Q - 1)
                hidden(n, q, 1)
                hidden_hi(n, q, 1)
                if below(e, E - 1) or q < Q - 1:
                    slots_hi(n + 1, (q + 1) % Q)
                hidden(n, q, 2)
                hidden_hi(n, q, 2)
                hidden(n, q, 3)
                hidden_hi(n, q, 3)

            steps(act, body)
            out_half(E * Q - 1, E - 1, 1, Q - 1)

        @block.vector
        def _(dve):
            def weight_parts(e, es, k):
                dve.wait_ge(w_ld[k], 16 * (e + 1))
                wait(dve, y_done, Q * (e - 1))
                dve.tensor_copy(whi[k][es][:, :], raw[k][:, :]).then_inc(whi_done, 1)
                dve.wait_ge(whi_done, 3 * e + k + 1)
                dve.tensor_tensor(wlo[k][es][:, :], raw[k][:, :], whi[k][es][:, :].bitcast(fp32),
                                  ALU.subtract).then_inc(wlo_done, 1)

            def shares(e, es):
                wait(dve, ya_done, Q * (e - 1))
                wait(dve, yb_done, Q * (e - 1))
                dve.tensor_copy(w_e[es][:, :], wts[:, bass.ds(e, 1), :]).then_inc(we_done, 1)

            def slots_lo(n, q):
                dve.wait_ge(xhi_done, n + 1)
                wait(dve, gu_done, FC * (n - 1))
                dve.tensor_tensor(xlo[q % 2][:, :, :], x_ps[:, :, :], xhi[q % 2][:, :, :].bitcast(fp32),
                                  ALU.subtract).then_inc(xlo_done, 1)

            def product(n, q, f):
                dve.wait_ge(gelu_done, FC * n + f + 1)
                wait(dve, hlo_done, FC * n + f - 1)
                dve.tensor_tensor(hid[f % 2][:, :], u_ps[f % 2][:, :], act_g[f % 2][:, :],
                                  ALU.mult).then_inc(hid_done, 1)

            def out_half(n, e, es, q):
                dve.wait_ge(ya_done, n + 1)
                dve.wait_ge(we_done, e + 1)
                for r in range(R // 2, R):
                    last = dve.tensor_scalar(yo[q % 2][:, r, :], y_ps[:, r, :], w_e[es][:, q * R + r:q * R + r + 1],
                                             None, ALU.mult)
                last.then_inc(yb_done, 1)

            shares(0, 0)
            for k in range(3):
                weight_parts(0, 0, k)
            slots_lo(0, 0)

            def body(e, es, q):
                n = Q * e + q
                product(n, q, 0)
                if q > 0:
                    out_half(n - 1, e, es, q - 1)
                elif at_least(e, 1):
                    out_half(n - 1, e - 1, 1 - es, Q - 1)
                product(n, q, 1)
                if below(e, E - 1) or q < Q - 1:
                    slots_lo(n + 1, (q + 1) % Q)
                product(n, q, 2)
                product(n, q, 3)
                if below(e, E - 1):
                    if q == 0:
                        shares(e + 1, 1 - es)
                    else:
                        weight_parts(e + 1, 1 - es, q - 1)

            steps(dve, body)
            out_half(E * Q - 1, E - 1, 1, Q - 1)


def shared_phase(nc, sem, xn_d, x1_d, sg, su, sd, idx_col, eo_d, out):
    Q = 4
    N = Q * S
    STEPS = B // Q
    HALF = E * CAP // P
    with ExitStack() as ctx:
        def sb(name, shape, dt=fp32):
            return ctx.enter_context(nc.sbuf_tensor(name, shape, dt))

        def pb(name, shape):
            return ctx.enter_context(nc.psum_tensor(name, shape, fp32))

        ident = sb("s_ident", [P, P])
        tok_i = sb("s_tok_i", [P, S], u32)
        tok = sb("s_tok", [P, S])
        raw = [sb(f"s_raw{k}", [P, DC * F]) for k in range(3)]
        whi = [sb(f"s_whi{k}", [P, DC * F], f32r) for k in range(3)]
        wlo = [sb(f"s_wlo{k}", [P, DC * F], f32r) for k in range(3)]
        xg = [sb(f"s_x{s}", [P, Q, D]) for s in range(2)]
        res = [sb(f"s_res{s}", [P, Q, D]) for s in range(2)]
        eo = [sb(f"s_eo{s}", [P, HALF, Q, D]) for s in range(2)]
        hot = [sb(f"s_hot{s}", [P, HALF, Q, S]) for s in range(2)]
        xhi = [sb(f"s_xhi{s}", [P, DC, N], f32r) for s in range(2)]
        xlo = [sb(f"s_xlo{s}", [P, DC, N], f32r) for s in range(2)]
        act_g = [sb(f"s_g{s}", [P, N]) for s in range(2)]
        hid = [sb(f"s_h{s}", [P, N]) for s in range(2)]
        hhi = [sb(f"s_hhi{s}", [P, FC, N], f32r) for s in range(2)]
        hlo = [sb(f"s_hlo{s}", [P, FC, N], f32r) for s in range(2)]
        yo = [sb(f"s_yo{s}", [P, Q, D]) for s in range(2)]
        x_ps = pb("s_x_ps", [P, DC, N])
        g_ps = [pb(f"s_g_ps{s}", [P, N]) for s in range(2)]
        u_ps = [pb(f"s_u_ps{s}", [P, N]) for s in range(2)]
        y_ps = pb("s_y_ps", [P, Q, D])

        ident0 = sem("s_ident0")
        ident_made = sem("s_ident_made")
        tok_made = sem("s_tok_made")
        tok_done = sem("s_tok_done")
        w_ld = [sem(f"s_w_ld{k}") for k in range(3)]
        whi_done = sem("s_whi_done")
        wlo_done = sem("s_wlo_done")
        x_ld = [sem(f"s_x_ld{s}") for s in range(2)]
        r_ld = [sem(f"s_r_ld{s}") for s in range(2)]
        eo_ld = [sem(f"s_eo_ld{s}") for s in range(2)]
        xt_done = sem("s_xt_done")
        xhi_done = sem("s_xhi_done")
        xlo_done = sem("s_xlo_done")
        hot_done = sem("s_hot_done")
        gu_done = sem("s_gu_done")
        gelu_done = sem("s_gelu_done")
        hid_done = sem("s_hid_done")
        hhi_done = sem("s_hhi_done")
        hlo_done = sem("s_hlo_done")
        y_done = sem("s_y_done")
        o_done = sem("s_o_done")
        o_st = [sem(f"s_o_st{s}") for s in range(2)]
        block = ctx.enter_context(nc.Block())

        def steps(eng, body):
            for n in range(4):
                body(n, n % 2)
            with eng.Fori(2, STEPS // 2 - 1) as i:
                for s in range(2):
                    body(2 * i + s, s)
            for n in range(STEPS - 2, STEPS):
                body(n, n % 2)

        def rounds(n, s):
            return n // 2 + 1 if isinstance(n, int) else (n - s) // 2 + 1

        eo_v = eo_d.rearrange("b (h e) r d -> (e r) h b d", h=HALF)

        @block.sync
        def _(sp):
            def load(n, s):
                rows = bass.ds(n * Q, Q)
                wait(sp, xt_done, n - 1)
                sp.dma_start(xg[s][:, :, :], xn_d[rows].rearrange("b t d -> t b d")).then_inc(x_ld[s], 16)
                wait(sp, y_done, n - 1)
                for half in range(HALF):
                    sp.dma_start(eo[s][:, half, :, :], eo_v[:, half, rows, :]).then_inc(eo_ld[s], 16)
                wait(sp, o_done, n - 1)
                sp.dma_start(res[s][:, :, :], x1_d[rows].rearrange("b t d -> t b d")).then_inc(r_ld[s], 16)

            for k, w in enumerate((sg, su, sd)):
                sp.dma_start(raw[k][:, :].rearrange("p (c n) -> p c n", c=D // P if k < 2 else F // P),
                             w.rearrange("(c p) n -> p c n", p=P)).then_inc(w_ld[k], 16)
            load(0, 0)
            load(1, 1)

            def body(n, s):
                sp.wait_ge(o_done, n + 1)
                sp.dma_start(out[bass.ds(n * Q, Q)].rearrange("b t d -> t b d"), yo[s][:, :, :]).then_inc(o_st[s], 16)
                if below(n, STEPS - 2):
                    load(n + 2, s)

            steps(sp, body)
            for s in range(2):
                sp.wait_ge(o_st[s], 16 * STEPS // 2)

        @block.gpsimd
        def _(pool):
            pool.memset(ident[:, :], 0.0).then_inc(ident0, 1)
            pool.iota(tok_i[:, :], pattern=[[1, S]], base=0, channel_multiplier=0).then_inc(tok_made, 1)
            pool.wait_ge(ident0, 1)
            pool.affine_select(out=ident[:, :], in_=ident[:, :], compare_op=ALU.not_equal, fill=1.0,
                               base=0, pattern=[[-1, P]], channel_multiplier=1).then_inc(ident_made, 1)

            def body(n, s):
                for f in range(FC):
                    ready, used = count(pool, FC * n + f + 1), count(pool, n - 1)
                    pool.wait_ge(hhi_done, ready)
                    if f == 0:
                        wait(pool, y_done, used)
                    pool.tensor_tensor(hlo[s][:, f, :], hid[f % 2][:, :], hhi[s][:, f, :].bitcast(fp32),
                                       ALU.subtract).then_inc(hlo_done, 1)

            steps(pool, body)

        @block.tensor
        def _(pe):
            pe.wait_ge(ident_made, 1)

            def tokens_T(n, s):
                pe.wait_ge(x_ld[s], 16 * rounds(n, s))
                wait(pe, xlo_done, n)
                for r in range(Q):
                    for c in range(DC):
                        last = pe.transpose(x_ps[:, c, r * P:(r + 1) * P], xg[s][:, r, c * P:(c + 1) * P],
                                            ident[:, :])
                last.then_inc(xt_done, 1)

            def up(n, s, f):
                if f == 0:
                    pe.wait_ge(xlo_done, n + 1)
                    pe.wait_ge(xhi_done, n + 1)
                wait(pe, hid_done, FC * n + f - 1)
                for k, bank in ((0, g_ps[f % 2]), (1, u_ps[f % 2])):
                    parts = [(w, x, c) for c in range(DC)
                             for w, x in ((whi, xhi), (whi, xlo), (wlo, xhi))]
                    for m, (w, x, c) in enumerate(parts):
                        last = pe.matmul(bank[:, :], w[k][:, c * F + f * P:c * F + (f + 1) * P],
                                         x[s][:, c, :], start=m == 0, stop=m == len(parts) - 1)
                last.then_inc(gu_done, 1)

            def down(n, s):
                pe.wait_ge(hlo_done, FC * (n + 1))
                pe.wait_ge(eo_ld[s], 16 * HALF * rounds(n, s))
                pe.wait_ge(hot_done, n + 1)
                wait(pe, o_done, n)
                for r in range(Q):
                    parts = [(h, w, f) for f in range(FC)
                             for h, w in ((hhi, whi), (hhi, wlo), (hlo, whi))]
                    for m, (h, w, f) in enumerate(parts):
                        pe.matmul(y_ps[:, r, :], h[s][:, f, r * P:(r + 1) * P],
                                  w[2][:, f * D:(f + 1) * D], start=m == 0, stop=False)
                    for half in range(HALF):
                        last = pe.matmul(y_ps[:, r, :], hot[s][:, half, r, :], eo[s][:, half, r, :],
                                         start=False, stop=half == HALF - 1)
                last.then_inc(y_done, 1)

            pe.wait_ge(wlo_done, 3)
            tokens_T(0, 0)

            def body(n, s):
                up(n, s, 0)
                if at_least(n, 1):
                    down(n - 1, 1 - s)
                up(n, s, 1)
                if below(n, STEPS - 1):
                    tokens_T(n + 1, 1 - s)
                up(n, s, 2)
                up(n, s, 3)

            steps(pe, body)
            down(STEPS - 1, 1)

        @block.scalar
        def _(act):
            def tokens_hi(n, s):
                act.wait_ge(xt_done, n + 1)
                wait(act, gu_done, FC * (n - 1))
                act.activation(xhi[s][:, :, :], x_ps[:, :, :], ACT.Copy).then_inc(xhi_done, 1)

            def hidden(n, s, f):
                act.wait_ge(gu_done, FC * n + f + 1)
                wait(act, hid_done, FC * n + f - 1)
                act.activation(act_g[f % 2][:, :], g_ps[f % 2][:, :], ACT.Gelu).then_inc(gelu_done, 1)

            def hidden_hi(n, s, f):
                act.wait_ge(hid_done, FC * n + f + 1)
                if f == 0:
                    wait(act, y_done, n - 1)
                act.activation(hhi[s][:, f, :], hid[f % 2][:, :], ACT.Copy).then_inc(hhi_done, 1)

            tokens_hi(0, 0)

            def body(n, s):
                hidden(n, s, 0)
                hidden_hi(n, s, 0)
                hidden(n, s, 1)
                hidden_hi(n, s, 1)
                if below(n, STEPS - 1):
                    tokens_hi(n + 1, 1 - s)
                hidden(n, s, 2)
                hidden_hi(n, s, 2)
                hidden(n, s, 3)
                hidden_hi(n, s, 3)

            steps(act, body)

        @block.vector
        def _(dve):
            for k in range(3):
                dve.wait_ge(w_ld[k], 16)
                dve.tensor_copy(whi[k][:, :], raw[k][:, :]).then_inc(whi_done, 1)
                dve.wait_ge(whi_done, k + 1)
                dve.tensor_tensor(wlo[k][:, :], raw[k][:, :], whi[k][:, :].bitcast(fp32),
                                  ALU.subtract).then_inc(wlo_done, 1)
            dve.wait_ge(tok_made, 1)
            dve.tensor_copy(tok[:, :], tok_i[:, :]).then_inc(tok_done, 1)
            dve.wait_ge(tok_done, 1)

            def tokens_lo(n, s):
                dve.wait_ge(xhi_done, n + 1)
                wait(dve, gu_done, FC * (n - 1))
                dve.tensor_tensor(xlo[s][:, :, :], x_ps[:, :, :], xhi[s][:, :, :].bitcast(fp32),
                                  ALU.subtract).then_inc(xlo_done, 1)

            def one_hot(n, s):
                wait(dve, y_done, n - 1)
                for half in range(HALF):
                    last = dve.tensor_tensor(
                        hot[s][:, half, :, :], tok[:, :].rearrange("p (o t) -> p o t", o=1).to_broadcast([P, Q, S]),
                        idx_col[:, half, bass.ds(n * Q, Q)].rearrange("p (b o) -> p b o", o=1)
                        .to_broadcast([P, Q, S]), ALU.is_equal)
                last.then_inc(hot_done, 1)

            def product(n, s, f):
                dve.wait_ge(gelu_done, FC * n + f + 1)
                wait(dve, hlo_done, FC * n + f - 1)
                dve.tensor_tensor(hid[f % 2][:, :], u_ps[f % 2][:, :], act_g[f % 2][:, :],
                                  ALU.mult).then_inc(hid_done, 1)

            def finish(n, s):
                dve.wait_ge(y_done, n + 1)
                dve.wait_ge(r_ld[s], 16 * rounds(n, s))
                if at_least(n, 2):
                    dve.wait_ge(o_st[s], 16 * (rounds(n, s) - 1))
                dve.tensor_tensor(yo[s][:, :, :], y_ps[:, :, :], res[s][:, :, :], ALU.add).then_inc(o_done, 1)

            tokens_lo(0, 0)

            def body(n, s):
                product(n, s, 0)
                if at_least(n, 1):
                    finish(n - 1, 1 - s)
                product(n, s, 1)
                if below(n, STEPS - 1):
                    tokens_lo(n + 1, 1 - s)
                product(n, s, 2)
                one_hot(n, s)
                product(n, s, 3)

            steps(dve, body)
            finish(STEPS - 1, 1)


def program(nc, x, ctx_in, wq, bq, wk, bk, wv, bv, rel, gate, wg, wu, wd, sg, su, sd, out):
    x1_d = nc.dram_tensor("x1_rows", [B, S, D], fp32).ap()
    xn_d = nc.dram_tensor("normed_rows", [B, S, D], fp32).ap()
    lg_d = nc.dram_tensor("router_logits", [B, E, S], fp32).ap()
    eo_d = nc.dram_tensor("expert_outputs", [B, E, CAP, D], fp32).ap()
    with ExitStack() as ctx:
        def sem(name):
            return ctx.enter_context(nc.semaphore(name))

        attention_phase(nc, sem, x, ctx_in, wq, wk, wv, bq, bk, bv, rel, gate, x1_d, xn_d, lg_d)
        gidx = ctx.enter_context(nc.sbuf_tensor("gidx", [P, E * CAP], u32))
        wts = ctx.enter_context(nc.sbuf_tensor("wts", [P, E, CAP], fp32))
        idx_col = ctx.enter_context(nc.sbuf_tensor("idx_col", [P, E * CAP // P, B], fp32))
        routing_phase(nc, sem, lg_d, gidx, wts, idx_col)
        expert_phase(nc, sem, xn_d.rearrange("b t d -> (b t) d"), wg, wu, wd, gidx, wts, eo_d)
        shared_phase(nc, sem, xn_d, x1_d, sg, su, sd, idx_col, eo_d, out)


_INS = ["x", "ctx_1024", "L0_xattn_Wq", "L0_xattn_bq", "L0_xattn_Wk", "L0_xattn_bk", "L0_xattn_Wv", "L0_xattn_bv",
        "L0_xattn_rel_emb", "L0_ffn_gate_w", "L0_ffn_Wg", "L0_ffn_Wu", "L0_ffn_Wd", "L0_ffn_Ws_g", "L0_ffn_Ws_u",
        "L0_ffn_Ws_d"]


def kernel(**inputs):
    import numpy as np
    import concourse.bacc as bacc
    from concourse.bass_utils import run_bass_kernel_spmd as run

    laid = {n: np.ascontiguousarray(inputs[n]) for n in _INS}
    for n in _INS[9:]:
        laid[n] = np.ascontiguousarray(np.swapaxes(laid[n], -1, -2))
    rel = laid["L0_xattn_rel_emb"]
    n_rel = rel.shape[1]
    at = [j + n_rel if j < 0 else min(j, n_rel - 1) for j in range(MAXLEN - S, MAXLEN - S + RELS)]
    laid["L0_xattn_rel_emb"] = np.ascontiguousarray(rel[:, at[::-1]])
    nc = bacc.Bacc("TRN2", target_bir_lowering=False, num_devices=1)
    args = [nc.dram_tensor(f"in_{n}", laid[n].shape, mybir.dt.from_np(laid[n].dtype), kind="ExternalInput").ap()
            for n in _INS]
    out = nc.dram_tensor("out_0", (B, S, D), fp32, kind="ExternalOutput").ap()
    program(nc, *args, out)
    r = run(nc, [{f"in_{n}": laid[n] for n in _INS}], core_ids=[0])
    return r.results[0]["out_0"]
```

```python
import concourse.bass as bass
from concourse import mybir
from contextlib import ExitStack

B, S, D = 128, 128, 256
H = 16
DK = D // H
E = 16
F = 512
CAP = S * 2 // E
P = 128
DC = D // P
FC = F // P
G = 4
GH = H // G
VW = DK + 1
AVW = 64
EPS = 1e-5
LOWEST = -3.0e38
MAXLEN = 125
RELS = 2 * S - 1

fp32 = mybir.dt.float32
f32r = mybir.dt.float32r
u32 = mybir.dt.uint32
ALU = mybir.AluOpType
ACT = mybir.ActivationFunctionType
AX = mybir.AxisListType


def head_of(group, j):
    return GH * group + j


def wait(eng, sem, n):
    if not (isinstance(n, int) and n <= 0):
        eng.wait_ge(sem, n)


def count(eng, n):
    if not isinstance(n, int):
        eng.compute_val(n)
    return n


def batches(eng, body):
    for b in range(8):
        body(b, b % 4)
    with eng.Fori(2, B // 4 - 1) as i:
        for s in range(4):
            body(4 * i + s, s)
    for b in range(B - 4, B):
        body(b, b % 4)


def at_least(b, n):
    return not isinstance(b, int) or b >= n


def below(b, n):
    return not isinstance(b, int) or b < n


def attention_phase(nc, sem, x, ctx_in, wq, wk, wv, bq, bk, bv, rel, gate, x1_d, xn_d, lg_d):
    with ExitStack() as ctx:
        def sb(name, shape, dt=fp32):
            return ctx.enter_context(nc.sbuf_tensor(name, shape, dt))

        def pb(name, shape):
            return ctx.enter_context(nc.psum_tensor(name, shape, fp32))

        ident = sb("a_ident", [P, P])
        flip = sb("flip", [P, P])
        wq_s = sb("wq_s", [P, DC, D])
        wk_s = sb("wk_s", [P, DC, D])
        wv_s = sb("wv_s", [P, DC, D])
        gate_s = sb("gate_s", [P, DC, E])
        bq_s = sb("bq_s", [P, DC])
        bk_s = sb("bk_s", [P, DC])
        bv_row = sb("bv_row", [1, D])
        bv_all = sb("bv_all", [P, D])
        bias_in = sb("bias_in", [P, H, S])
        nbias = sb("nbias", [P, G, GH, S])
        parity = sb("parity", [P, 2])
        ppow = sb("ppow", [P, 1])
        epsc = sb("epsc", [P, 1])
        xt = [sb(f"xt{s}", [P, D]) for s in range(2)]
        ct = [sb(f"ct{s}", [P, DC, S]) for s in range(2)]
        xb = [sb(f"xb{s}", [P, D]) for s in range(4)]
        xn = [sb(f"xn{s}", [P, D]) for s in range(2)]
        st1 = [sb(f"st1{s}", [P, 6]) for s in range(2)]
        mv1 = [sb(f"mv1{s}", [P, 2]) for s in range(2)]
        rs1 = [sb(f"rs1{s}", [P, 2]) for s in range(2)]
        xT = [sb(f"xT{s}", [P, DC, P]) for s in range(2)]
        qm = [sb(f"qm{s}", [P, DC, 2, P]) for s in range(2)]
        kT = [sb(f"kT{s}", [P, DC, P]) for s in range(2)]
        v1 = [sb(f"v1{s}", [P, H * VW + AVW]) for s in range(2)]
        sc = [sb(f"sc{s}", [P, G, GH, S]) for s in range(2)]
        nmax = [sb(f"nmax{s}", [P, G, GH]) for s in range(2)]
        pr = [sb(f"pr{s}", [P, G, GH, S]) for s in range(2)]
        pT = [sb(f"pT{s}", [P, G, GH, S]) for s in range(2)]
        rinv = [sb(f"rinv{s}", [P, H]) for s in range(2)]
        att = [sb(f"att{s}", [P, D]) for s in range(2)]
        x1 = [sb(f"x1{s}", [P, D]) for s in range(2)]
        st2 = [sb(f"st2{s}", [P, 6]) for s in range(2)]
        mv2 = [sb(f"mv2{s}", [P, 2]) for s in range(2)]
        rs2 = [sb(f"rs2{s}", [P, 2]) for s in range(2)]
        x2 = [sb(f"x2{s}", [P, D]) for s in range(2)]
        x2T = [sb(f"x2T{s}", [P, DC, P]) for s in range(2)]
        lg = [sb(f"lg{s}", [P, E]) for s in range(2)]

        s_ps = [pb(f"s_ps{g}", [P, GH, S]) for g in range(G)]
        front = pb("front", [P, 4, P])
        ring = [pb(f"ring{k}", [P, 4, P]) for k in range(2)]
        o_ps = pb("o_ps", [P, H * VW + AVW + E])
        o_heads = o_ps[:, 0:H * VW].rearrange("p (h d) -> p h d", d=VW)
        o_logits = o_ps[:, H * VW + AVW:H * VW + AVW + E]

        N_CONST = 2 * DC * DC + 2 * G + 3 + H
        const_ld = sem("const_ld")
        ident0 = sem("ident0")
        par0 = sem("par0")
        flip_made = sem("flip_made")
        flipped = sem("flipped")
        const_pool = sem("const_pool")
        const_dve = sem("const_dve")
        x_ld = [sem(f"x_ld{s}") for s in range(2)]
        c_ld = [sem(f"c_ld{s}") for s in range(2)]
        xb_done = sem("xb_done")
        stats1 = sem("stats1")
        var1 = sem("var1")
        eps1 = sem("eps1")
        rstd1 = sem("rstd1")
        xn_done = sem("xn_done")
        t_done = sem("t_done")
        xT_done = sem("xT_done")
        qk_done = sem("qk_done")
        v_done = sem("v_done")
        q_done = sem("q_done")
        kT_done = sem("kT_done")
        v1_done = sem("v1_done")
        s_done = sem("s_done")
        max_done = sem("max_done")
        exp_done = sem("exp_done")
        pt_done = sem("pt_done")
        pT_done = sem("pT_done")
        av_done = sem("av_done")
        rinv_done = sem("rinv_done")
        att_done = sem("att_done")
        x1_done = sem("x1_done")
        stats2 = sem("stats2")
        var2 = sem("var2")
        eps2 = sem("eps2")
        rstd2 = sem("rstd2")
        x2_done = sem("x2_done")
        x2t_done = sem("x2t_done")
        x2T_done = sem("x2T_done")
        lgp_done = sem("lgp_done")
        lg_done = sem("lg_done")
        x1_st = [sem(f"x1_st{s}") for s in range(2)]
        x2_st = [sem(f"x2_st{s}") for s in range(2)]
        lg_st = [sem(f"lg_st{s}") for s in range(2)]

        def rounds(b, s):
            return b // 2 + 1 if isinstance(b, int) else (b - s % 2) // 2 + 1

        block = ctx.enter_context(nc.Block())

        @block.sync
        def _(sp):
            n_const = 0
            for m in range(DC):
                for dst, src in ((wq_s, wq), (wk_s, wk)):
                    for c in range(DC):
                        sp.dma_start(dst[:, c, m * P:(m + 1) * P].rearrange("p (g r) -> p g r", g=G),
                                     src[c * P:(c + 1) * P].rearrange("p (g m r) -> p m g r", g=G, m=DC)[:, m]
                                     ).then_inc(const_ld, 16)
            sp.dma_start(wv_s[:, :, :], wv.rearrange("(c p) n -> p c n", p=P)).then_inc(const_ld, 16)
            sp.dma_start(gate_s[:, :, :], gate.rearrange("(c p) n -> p c n", p=P)).then_inc(const_ld, 16)
            with nc.allow_non_contiguous_dma(reason="a bias vector is spread over the partitions once"):
                for dst, src in ((bq_s, bq), (bk_s, bk)):
                    for g in range(G):
                        sp.dma_start(dst[32 * g:32 * g + 32, :], src.rearrange("(g m r) -> g r m", g=G, m=DC)[g]
                                     ).then_inc(const_ld, 16)
            sp.dma_start(bv_row[:, :], bv.rearrange("(a n) -> a n", a=1)).then_inc(const_ld, 16)
            for h in range(H):
                win = bass.AP(rel.tensor, h * RELS, [[1, P], [1, S]])
                sp.dma_start(bias_in[:, h, :], win).then_inc(const_ld, 16)

            def load_x(b, s):
                wait(sp, xn_done, b - 1)
                wait(sp, xb_done, b - 1)
                sp.dma_start(xt[s % 2][:, :], x[b]).then_inc(x_ld[s % 2], 16)

            def load_ctx(b, s):
                wait(sp, v_done, b - 1)
                sp.dma_start(ct[s % 2][:, :, :], ctx_in[b].rearrange("(c p) t -> p c t", p=P)
                             ).then_inc(c_ld[s % 2], 16)

            for b in range(2):
                load_x(b, b)
                load_ctx(b, b)
            load_x(2, 2)
            load_x(3, 3)

            def store_rows(b, s):
                sp.wait_ge(x1_done, b + 1)
                sp.dma_start(x1_d[b], x1[s % 2][:, :]).then_inc(x1_st[s % 2], 16)
                sp.wait_ge(x2_done, b + 1)
                sp.dma_start(xn_d[b], x2[s % 2][:, :]).then_inc(x2_st[s % 2], 16)

            def store_logits(b, s):
                sp.wait_ge(lg_done, b + 1)
                sp.dma_start(lg_d[b], lg[s % 2][:, :]).then_inc(lg_st[s % 2], 16)

            def body(b, s):
                if below(b, B - 4):
                    load_x(b + 4, s)
                if below(b, B - 2):
                    load_ctx(b + 2, s + 2)
                if at_least(b, 1):
                    store_rows(b - 1, s - 1)
                if at_least(b, 3):
                    store_logits(b - 3, s - 3)

            batches(sp, body)
            store_rows(B - 1, 3)
            for b in range(B - 3, B):
                store_logits(b, b % 4)
            for s in range(2):
                for done in (x1_st[s], x2_st[s], lg_st[s]):
                    sp.wait_ge(done, 16 * B // 2)

        @block.gpsimd
        def _(pool):
            pool.memset(ident[:, :], 0.0).then_inc(ident0, 1)
            pool.memset(flip[:, :], 0.0).then_inc(ident0, 1)
            pool.memset(parity[:, :], 0.0).then_inc(par0, 1)
            pool.memset(ppow[:, :], -0.5)
            pool.memset(epsc[:, :], EPS)
            pool.wait_ge(ident0, 2)
            pool.affine_select(out=flip[:, :], in_=flip[:, :], compare_op=ALU.not_equal, fill=-1.0,
                               base=1 - P, pattern=[[1, P]], channel_multiplier=1).then_inc(flip_made, 1)
            pool.affine_select(out=ident[:, :], in_=ident[:, :], compare_op=ALU.not_equal, fill=1.0,
                               base=0, pattern=[[-1, P]], channel_multiplier=1).then_inc(const_pool, 1)
            pool.wait_ge(const_ld, 16 * N_CONST)
            pool.partition_broadcast(bv_all[:, :], bv_row[0:1, :], channels=P).then_inc(const_pool, 1)
            pool.wait_ge(const_pool, 2)

            def keep_residual(b, s):
                pool.wait_ge(x_ld[s % 2], 16 * rounds(b, s))
                wait(pool, x1_done, b - 3)
                pool.tensor_tensor(xb[s % 4][:, :], xt[s % 2][:, :], bv_all[:, :], ALU.add).then_inc(xb_done, 1)

            def inverse_root(b, s, stats, mv, rs, eps, rstd):
                pool.wait_ge(stats, b + 1)
                pool.tensor_tensor(rs[s % 2][:, 1:2], mv[s % 2][:, 1:2], epsc[:, :], ALU.add).then_inc(eps, 1)
                pool.wait_ge(eps, b + 1)
                pool.tensor_tensor(rs[s % 2][:, 0:1], rs[s % 2][:, 1:2], ppow[:, :], ALU.pow).then_inc(rstd, 1)

            for b in range(3):
                keep_residual(b, b)
                inverse_root(b, b, stats1, mv1, rs1, eps1, rstd1)

            def residual(b, s):
                pool.wait_ge(att_done, b + 1)
                if at_least(b, 2):
                    pool.wait_ge(x1_st[s % 2], 16 * (rounds(b, s) - 1))
                pool.tensor_tensor(x1[s % 2][:, :], att[s % 2][:, :], xb[s % 4][:, :], ALU.add).then_inc(x1_done, 1)

            def second_norm(b, s):
                inverse_root(b, s, stats2, mv2, rs2, eps2, rstd2)
                ready, used, stored = count(pool, b + 1), count(pool, b - 1), count(pool, 16 * (rounds(b, s) - 1))
                pool.wait_ge(const_pool, 2)
                pool.wait_ge(rstd2, ready)
                wait(pool, x2t_done, used)
                wait(pool, x2_st[s % 2], stored)
                pool.tensor_scalar(x2[s % 2][:, :], x1[s % 2][:, :], mv2[s % 2][:, 0:1], rs2[s % 2][:, 0:1],
                                   ALU.subtract, ALU.mult).then_inc(x2_done, 1)

            def body(b, s):
                if at_least(b, 1):
                    residual(b - 1, s - 1)
                if below(b, B - 3):
                    keep_residual(b + 3, s + 3)
                    inverse_root(b + 3, s + 3, stats1, mv1, rs1, eps1, rstd1)
                if at_least(b, 1):
                    second_norm(b - 1, s - 1)

            batches(pool, body)
            residual(B - 1, 3)
            second_norm(B - 1, 3)

        @block.tensor
        def _(pe):
            pe.wait_ge(const_ld, 16 * N_CONST)
            pe.wait_ge(const_pool, 1)
            pe.wait_ge(flip_made, 1)
            for g in range(G):
                for j in range(GH):
                    last = pe.matmul(s_ps[g][:, j, :], flip[:, :], bias_in[:, head_of(g, j), :], start=True, stop=True)
            last.then_inc(flipped, 1)

            def transposes(b, s):
                pe.wait_ge(xn_done, b + 1)
                wait(pe, v1_done, b - 1)
                wait(pe, x2T_done, b - 4)
                for c in range(DC):
                    last = pe.transpose(front[:, c, :], xn[s % 2][:, c * P:(c + 1) * P], ident[:, :])
                last.then_inc(t_done, 1)

            def project_qk(b, s):
                pe.wait_ge(c_ld[s % 2], 16 * rounds(b, s))
                pe.wait_ge(xT_done, b + 1)
                for w, src, o in ((wq_s, xT, 0), (wk_s, ct, DC)):
                    for m in range(DC):
                        for c in range(DC):
                            last = pe.matmul(front[:, o + m, :], w[:, c, m * P:(m + 1) * P],
                                             src[s % 2][:, c, :], start=c == 0, stop=c == DC - 1)
                last.then_inc(qk_done, 1)

            def project_v(b, s):
                wait(pe, kT_done, b + 2 if below(b, B - 1) else B)
                out = front[:, 0:DC, :].rearrange("p a n -> p (a n)")
                for c in range(DC):
                    last = pe.matmul(out, ct[s % 2][:, c, :], wv_s[:, c, :], start=c == 0, stop=c == DC - 1)
                last.then_inc(v_done, 1)

            def rows_T(b, s):
                pe.wait_ge(x2_done, b + 1)
                for c in range(DC):
                    last = pe.transpose(front[:, DC + c, :], x2[s % 2][:, c * P:(c + 1) * P], ident[:, :])
                last.then_inc(x2t_done, 1)

            def scores(b, s, pair):
                wait(pe, max_done, H * (b - 1) + 2 * GH * (pair + 1))
                if pair == 0:
                    if isinstance(b, int) and b == 0:
                        pe.wait_ge(const_dve, 6)
                    pe.wait_ge(q_done, 4 * (b + 1))
                    pe.wait_ge(kT_done, b + 1)
                for j in range(GH):
                    for g in (2 * pair, 2 * pair + 1):
                        rows = slice(32 * g, 32 * g + 32)
                        last = pe.matmul(s_ps[g][:, j, :], qm[s % 2][rows, j // 2, j % 2, :],
                                         kT[s % 2][rows, j // 2, :], start=True, stop=True)
                last.then_inc(s_done, 1)

            def probs_T(b, s, g):
                pe.wait_ge(exp_done, H * b + GH * (g + 1))
                wait(pe, pT_done, 4 * b + g - 1)
                for j in range(GH):
                    last = pe.transpose(ring[g % 2][:, j, :], pr[s % 2][:, g, j, :], ident[:, :])
                last.then_inc(pt_done, 1)

            def weigh_values(b, s, g):
                pe.wait_ge(pT_done, 4 * b + g + 1)
                if g == 0:
                    pe.wait_ge(v1_done, b + 1)
                    wait(pe, att_done, b)
                for j in range(GH):
                    at = head_of(g, j) * VW
                    last = pe.matmul(o_ps[:, at:at + AVW], pT[s % 2][:, g, j, :], v1[s % 2][:, at:at + AVW],
                                     start=True, stop=True)
                if g == G - 1:
                    last.then_inc(av_done, 1)

            def logits(b, s):
                pe.wait_ge(x2T_done, b + 1)
                for c in range(DC):
                    last = pe.matmul(o_logits, x2T[s % 2][:, c, :], gate_s[:, c, :], start=c == 0, stop=c == DC - 1)
                last.then_inc(lgp_done, 1)

            transposes(0, 0)
            project_qk(0, 0)
            pe.wait_ge(kT_done, 1)
            out = front[:, 0:DC, :].rearrange("p a n -> p (a n)")
            for c in range(DC):
                last = pe.matmul(out, ct[0][:, c, :], wv_s[:, c, :], start=c == 0, stop=c == DC - 1)
            last.then_inc(v_done, 1)
            scores(0, 0, 0)
            scores(0, 0, 1)
            pe.wait_ge(v1_done, 1)
            transposes(1, 1)
            project_qk(1, 1)

            def body(b, s):
                if at_least(b, 1):
                    weigh_values(b - 1, s - 1, G - 1)
                if below(b, B - 2):
                    pe.wait_ge(kT_done, b + 2)
                    transposes(b + 2, s + 2)
                if below(b, B - 1):
                    scores(b + 1, s + 1, 0)
                probs_T(b, s, 0)
                if below(b, B - 2):
                    project_qk(b + 2, s + 2)
                probs_T(b, s, 1)
                weigh_values(b, s, 0)
                probs_T(b, s, 2)
                weigh_values(b, s, 1)
                if below(b, B - 1):
                    project_v(b + 1, s + 1)
                if at_least(b, 2):
                    rows_T(b - 2, s - 2)
                if below(b, B - 1):
                    scores(b + 1, s + 1, 1)
                probs_T(b, s, 3)
                weigh_values(b, s, 2)
                if at_least(b, 2):
                    logits(b - 2, s - 2)

            batches(pe, body)
            weigh_values(B - 1, 3, G - 1)
            for b in range(B - 2, B):
                pe.wait_ge(x2T_done, b)
                rows_T(b, b % 4)
                pe.wait_ge(att_done, B)
                pe.wait_ge(lg_done, b)
                logits(b, b % 4)

        @block.scalar
        def _(act):
            def front_T(b, s):
                act.wait_ge(t_done, b + 1)
                wait(act, qk_done, b - 1)
                act.activation(xT[s % 2][:, :, :], front[:, 0:DC, :], ACT.Copy).then_inc(xT_done, 1)

            def keys(b, s):
                act.wait_ge(q_done, 4 * (b + 1))
                wait(act, s_done, 2 * (b - 1))
                for c in range(DC):
                    last = act.activation(kT[s % 2][:, c, :], front[:, DC + c, :], ACT.Identity,
                                          bias=bk_s[:, c:c + 1])
                last.then_inc(kT_done, 1)

            def values(b, s):
                act.wait_ge(v_done, b + 1)
                wait(act, x2t_done, b - 2)
                wait(act, av_done, b - 1)
                act.activation(v1[s % 2][:, 0:H * VW].rearrange("p (h d) -> p h d", d=VW)[:, :, 0:DK],
                               front[:, 0:DC, :].rearrange("p a (h d) -> p (a h) d", d=DK),
                               ACT.Copy).then_inc(v1_done, 1)

            def rows(b, s):
                act.wait_ge(x2t_done, b + 1)
                wait(act, lgp_done, b - 1)
                act.activation(x2T[s % 2][:, :, :], front[:, DC:2 * DC, :], ACT.Copy).then_inc(x2T_done, 1)

            def exps(b, s, g):
                wait(act, pt_done, 4 * (b - 2) + g + 1)
                for j in range(GH):
                    act.wait_ge(max_done, H * b + GH * g + j + 1)
                    act.activation(pr[s % 2][:, g, j, :], sc[s % 2][:, g, j, :], ACT.Exp,
                                   bias=nmax[s % 2][:, g, j:j + 1], scale=-1.0).then_inc(exp_done, 1)

            front_T(0, 0)
            act.wait_ge(const_ld, 16 * N_CONST)
            keys(0, 0)
            act.wait_ge(const_dve, 3)
            values(0, 0)
            front_T(1, 1)
            keys(1, 1)

            def body(b, s):
                exps(b, s, 0)
                if below(b, B - 2):
                    front_T(b + 2, s + 2)
                exps(b, s, 1)
                if below(b, B - 2):
                    keys(b + 2, s + 2)
                exps(b, s, 2)
                exps(b, s, 3)
                if below(b, B - 1):
                    values(b + 1, s + 1)
                if at_least(b, 2):
                    rows(b - 2, s - 2)

            batches(act, body)
            rows(B - 2, 2)
            rows(B - 1, 3)

        @block.vector
        def _(dve):
            for s in range(2):
                dve.memset(v1[s][:, H * VW:], 0.0)
                dve.memset(v1[s][:, 0:H * VW].rearrange("p (h d) -> p h d", d=VW)[:, :, DK:VW], 1.0
                           ).then_inc(const_dve, 1)
            dve.wait_ge(const_pool, 2)
            dve.wait_ge(par0, 1)
            blocks = ident[:, :].rearrange("p (a j d) -> p j a d", j=2, d=DK)
            for j in range(2):
                dve.tensor_reduce(parity[:, j:j + 1], blocks[:, j, :, :], AX.XY, ALU.add).then_inc(const_dve, 1)
            dve.wait_ge(const_dve, 4)
            dve.tensor_scalar(parity[:, :], parity[:, :], -float(DK) ** -0.5, None, ALU.mult).then_inc(const_dve, 1)
            dve.wait_ge(const_ld, 16 * N_CONST)
            dve.wait_ge(flipped, 1)
            for g in range(G):
                last = dve.tensor_copy(nbias[:, g, :, :], s_ps[g][:, :, :])
            last.then_inc(const_dve, 1)
            dve.wait_ge(const_dve, 6)

            def stats(src, b, s, st, mv, var, done):
                dve.bn_stats(st[s % 2][:, :], src[s % 2][:, :]).then_inc(var, 1)
                ready = count(dve, b + 1)
                dve.wait_ge(const_dve, 6)
                dve.wait_ge(var, ready)
                dve.bn_aggr(mv[s % 2][:, :], st[s % 2][:, :]).then_inc(done, 1)

            def stats_in(b, s):
                dve.wait_ge(x_ld[s % 2], 16 * rounds(b, s))
                wait(dve, rstd1, b - 1)
                stats(xt, b, s, st1, mv1, var1, stats1)

            def norm_in(b, s):
                dve.wait_ge(rstd1, b + 1)
                wait(dve, t_done, b - 1)
                dve.tensor_scalar(xn[s % 2][:, :], xt[s % 2][:, :], mv1[s % 2][:, 0:1], rs1[s % 2][:, 0:1],
                                  ALU.subtract, ALU.mult).then_inc(xn_done, 1)

            def queries(b, s):
                dve.wait_ge(qk_done, b + 1)
                wait(dve, s_done, 2 * (b - 1))
                for c in range(DC):
                    for j in range(2):
                        dve.tensor_scalar(qm[s % 2][:, c, j, :], front[:, c, :], bq_s[:, c:c + 1], parity[:, j:j + 1],
                                          ALU.add, ALU.mult).then_inc(q_done, 1)

            def add_bias_and_max(b, s, g):
                ready, used = count(dve, 2 * b + g // 2 + 1), count(dve, H * (b - 2) + GH * (g + 1))
                dve.wait_ge(const_dve, 6)
                dve.wait_ge(s_done, ready)
                wait(dve, exp_done, used)
                for j in range(GH):
                    dve.tensor_tensor_reduce(out=sc[s % 2][:, g, j, :], in0=s_ps[g][:, j, :], in1=nbias[:, g, j, :],
                                             scale=1.0, scalar=-LOWEST, op0=ALU.add, op1=ALU.min,
                                             accum_out=nmax[s % 2][:, g, j:j + 1]).then_inc(max_done, 1)

            def probs_out(b, s, g):
                dve.wait_ge(pt_done, 4 * b + g + 1)
                if g == 0:
                    wait(dve, av_done, b - 1)
                dve.tensor_copy(pT[s % 2][:, g, :, :], ring[g % 2][:, :, :]).then_inc(pT_done, 1)

            def normalise(b, s):
                dve.wait_ge(av_done, b + 1)
                wait(dve, x1_done, b - 1)
                dve.reciprocal(rinv[s % 2][:, :], o_heads[:, :, DK]).then_inc(rinv_done, 1)
                if at_least(b, 2):
                    logits_out(b - 2, s - 2)
                dve.wait_ge(rinv_done, b + 1)
                dve.tensor_tensor(att[s % 2][:, :].rearrange("p (h d) -> p h d", d=DK), o_heads[:, :, 0:DK],
                                  rinv[s % 2][:, :].rearrange("p (h o) -> p h o", o=1).to_broadcast([P, H, DK]),
                                  ALU.mult).then_inc(att_done, 1)

            def logits_out(b, s):
                dve.wait_ge(lgp_done, b + 1)
                if at_least(b, 2):
                    dve.wait_ge(lg_st[s % 2], 16 * (rounds(b, s) - 1))
                dve.tensor_copy(lg[s % 2][:, :], o_logits).then_inc(lg_done, 1)

            def stats_out(b, s):
                dve.wait_ge(x1_done, b + 1)
                wait(dve, x2_done, b - 1)
                stats(x1, b, s, st2, mv2, var2, stats2)

            for b in range(3):
                stats_in(b, b)
                norm_in(b, b)
                if b < 2:
                    queries(b, b)

            def body(b, s):
                add_bias_and_max(b, s, 0)
                if at_least(b, 1):
                    probs_out(b - 1, s - 1, 3)
                add_bias_and_max(b, s, 1)
                if at_least(b, 1):
                    normalise(b - 1, s - 1)
                add_bias_and_max(b, s, 2)
                probs_out(b, s, 0)
                add_bias_and_max(b, s, 3)
                if below(b, B - 2):
                    queries(b + 2, s + 2)
                if below(b, B - 3):
                    stats_in(b + 3, s + 3)
                probs_out(b, s, 1)
                if at_least(b, 1):
                    stats_out(b - 1, s - 1)
                probs_out(b, s, 2)
                if below(b, B - 3):
                    norm_in(b + 3, s + 3)

            batches(dve, body)
            probs_out(B - 1, 3, 3)
            normalise(B - 1, 3)
            stats_out(B - 1, 3)
            logits_out(B - 2, 2)
            logits_out(B - 1, 3)


def routing_phase(nc, sem, lg_d, gidx, wts, idx_col):
    HALF = E * CAP // P
    with ExitStack() as ctx:
        def sb(name, shape, dt=fp32):
            return ctx.enter_context(nc.sbuf_tensor(name, shape, dt))

        ident = sb("r_ident", [P, P])
        raw = sb("r_raw", [P, S, E])
        less = sb("r_less", [P, S, E])
        ex = sb("r_exp", [P, S, E])
        score = sb("r_score", [P, E, S])
        rest = sb("r_rest", [P, E, S])
        top = sb("r_max", [P, S])
        tot = sb("r_sum", [P, S])
        inv = sb("r_inv", [P, S])
        place = sb("r_place", [P, E, CAP], u32)
        place_f = sb("r_place_f", [P, E * CAP])
        first_row = sb("r_first_row", [P, 1], u32)
        first_row_f = sb("r_first_row_f", [P, 1])
        idx_ps = ctx.enter_context(nc.psum_tensor("r_idx_ps", [P, HALF, P], fp32))

        lg_ld = sem("r_lg_ld")
        zeroed = sem("r_zeroed")
        ident_made = sem("r_ident_made")
        rows_made = sem("r_rows_made")
        step = sem("r_step")
        exp_done = sem("r_exp_done")
        places = sem("r_places")
        turned = sem("r_turned")
        block = ctx.enter_context(nc.Block())

        @block.sync
        def _(sp):
            sp.dma_start(raw[:, :, :], lg_d[:, :, :]).then_inc(lg_ld, 16)

        @block.gpsimd
        def _(pool):
            pool.memset(ident[:, :], 0.0).then_inc(zeroed, 1)
            pool.iota(first_row[:, :], pattern=[[0, 1]], base=0, channel_multiplier=S).then_inc(rows_made, 1)
            pool.wait_ge(zeroed, 1)
            pool.affine_select(out=ident[:, :], in_=ident[:, :], compare_op=ALU.not_equal, fill=1.0,
                               base=0, pattern=[[-1, P]], channel_multiplier=1).then_inc(ident_made, 1)

        @block.scalar
        def _(act):
            act.wait_ge(step, 2)
            act.activation(ex[:, :, :], less[:, :, :], ACT.Exp).then_inc(exp_done, 1)

        @block.tensor
        def _(pe):
            pe.wait_ge(ident_made, 1)
            pe.wait_ge(places, 1)
            for half in range(HALF):
                last = pe.transpose(idx_ps[:, half, :], place_f[:, half * P:(half + 1) * P], ident[:, :])
            last.then_inc(turned, 1)

        @block.vector
        def _(dve):
            def per_token(t):
                return t[:, :].rearrange("p (t o) -> p t o", o=1).to_broadcast([P, S, E])

            dve.wait_ge(lg_ld, 16)
            dve.tensor_reduce(top[:, :], raw[:, :, :], AX.X, ALU.max).then_inc(step, 1)
            dve.wait_ge(step, 1)
            dve.tensor_tensor(less[:, :, :], raw[:, :, :], per_token(top), ALU.subtract).then_inc(step, 1)
            dve.wait_ge(exp_done, 1)
            dve.tensor_reduce(tot[:, :], ex[:, :, :], AX.X, ALU.add).then_inc(step, 1)
            dve.wait_ge(step, 3)
            dve.reciprocal(inv[:, :], tot[:, :]).then_inc(step, 1)
            dve.wait_ge(step, 4)
            dve.tensor_tensor(score[:, :, :].rearrange("p e t -> p t e"), ex[:, :, :], per_token(inv),
                              ALU.mult).then_inc(step, 1)
            dve.wait_ge(step, 5)
            for e in range(E):
                dve.max(wts[:, e, 0:8], score[:, e, :]).then_inc(step, 1)
            dve.wait_ge(step, 5 + E)
            for e in range(E):
                dve.max_index(place[:, e, 0:8], wts[:, e, 0:8], score[:, e, :]).then_inc(step, 1)
            for e in range(E):
                dve.match_replace(rest[:, e, :], wts[:, e, 0:8], score[:, e, :], -1.0).then_inc(step, 1)
            dve.wait_ge(step, 5 + 3 * E)
            for e in range(E):
                dve.max(wts[:, e, 8:16], rest[:, e, :]).then_inc(step, 1)
            dve.wait_ge(step, 5 + 4 * E)
            for e in range(E):
                dve.max_index(place[:, e, 8:16], wts[:, e, 8:16], rest[:, e, :]).then_inc(step, 1)
            dve.wait_ge(rows_made, 1)
            dve.wait_ge(step, 5 + 5 * E)
            dve.tensor_copy(place_f[:, :], place[:, :, :].rearrange("p e r -> p (e r)")).then_inc(places, 1)
            dve.tensor_copy(first_row_f[:, :], first_row[:, :]).then_inc(places, 1)
            dve.wait_ge(places, 2)
            dve.tensor_scalar(gidx[:, :], place_f[:, :], first_row_f[:, :], None, ALU.add)
            dve.wait_ge(turned, 1)
            dve.tensor_copy(idx_col[:, :, :], idx_ps[:, :, :])


def expert_phase(nc, sem, xn_rows, wg, wu, wd, gidx, wts, eo_d):
    Q = 4
    R = CAP // Q
    N = R * P
    with ExitStack() as ctx:
        def sb(name, shape, dt=fp32):
            return ctx.enter_context(nc.sbuf_tensor(name, shape, dt))

        def pb(name, shape):
            return ctx.enter_context(nc.psum_tensor(name, shape, fp32))

        ident = sb("e_ident", [P, P])
        raw = [sb(f"e_raw{k}", [P, DC * F]) for k in range(3)]
        whi = [[sb(f"e_whi{k}{s}", [P, DC * F], f32r) for s in range(2)] for k in range(3)]
        wlo = [[sb(f"e_wlo{k}{s}", [P, DC * F], f32r) for s in range(2)] for k in range(3)]
        idx_e = [sb(f"e_idx{s}", [P, CAP], u32) for s in range(2)]
        w_e = [sb(f"e_w{s}", [P, CAP]) for s in range(2)]
        xg = [sb(f"e_xg{s}", [P, R, D]) for s in range(2)]
        xhi = [sb(f"e_xhi{s}", [P, DC, N], f32r) for s in range(2)]
        xlo = [sb(f"e_xlo{s}", [P, DC, N], f32r) for s in range(2)]
        act_g = [sb(f"e_g{s}", [P, N]) for s in range(2)]
        hid = [sb(f"e_h{s}", [P, N]) for s in range(2)]
        hhi = [sb(f"e_hhi{s}", [P, FC, N], f32r) for s in range(2)]
        hlo = [sb(f"e_hlo{s}", [P, FC, N], f32r) for s in range(2)]
        yo = [sb(f"e_yo{s}", [P, R, D]) for s in range(2)]
        x_ps = pb("e_x_ps", [P, DC, N])
        g_ps = [pb(f"e_g_ps{s}", [P, N]) for s in range(2)]
        u_ps = [pb(f"e_u_ps{s}", [P, N]) for s in range(2)]
        y_ps = pb("e_y_ps", [P, R, D])

        ident0 = sem("e_ident0")
        ident_made = sem("e_ident_made")
        w_ld = [sem(f"e_w_ld{k}") for k in range(3)]
        whi_done = sem("e_whi_done")
        wlo_done = sem("e_wlo_done")
        idx_done = sem("e_idx_done")
        we_done = sem("e_we_done")
        xg_ld = [sem(f"e_xg_ld{s}") for s in range(2)]
        xt_done = sem("e_xt_done")
        xhi_done = sem("e_xhi_done")
        xlo_done = sem("e_xlo_done")
        gu_done = sem("e_gu_done")
        gelu_done = sem("e_gelu_done")
        hid_done = sem("e_hid_done")
        hhi_done = sem("e_hhi_done")
        hlo_done = sem("e_hlo_done")
        y_done = sem("e_y_done")
        ya_done = sem("e_ya_done")
        yb_done = sem("e_yb_done")
        y_st = [sem(f"e_y_st{s}") for s in range(2)]
        block = ctx.enter_context(nc.Block())

        w_src = [wg, wu, wd]

        def steps(eng, body):
            for e in range(2):
                for q in range(Q):
                    body(e, e % 2, q)
            with eng.Fori(1, E // 2 - 1) as i:
                for es in range(2):
                    for q in range(Q):
                        body(2 * i + es, es, q)
            for e in range(E - 2, E):
                for q in range(Q):
                    body(e, e % 2, q)

        def rounds(n, s):
            return n // 2 + 1 if isinstance(n, int) else (n - s) // 2 + 1

        @block.sync
        def _(sp):
            def load_weight(e, k):
                wait(sp, wlo_done, 3 * e + k - 2)
                sp.dma_start(raw[k][:, :].rearrange("p (c n) -> p c n", c=D // P if k < 2 else F // P),
                             w_src[k][e].rearrange("(c p) n -> p c n", p=P)).then_inc(w_ld[k], 16)

            for e in range(2):
                for k in range(3):
                    load_weight(e, k)

            def body(e, es, q):
                n = Q * e + q
                sp.wait_ge(ya_done, n + 1)
                sp.wait_ge(yb_done, n + 1)
                sp.dma_start(eo_d[:, e, q * R:(q + 1) * R, :], yo[q % 2][:, :, :]).then_inc(y_st[q % 2], 16)
                if q > 0 and below(e, E - 2):
                    load_weight(e + 2, q - 1)

            steps(sp, body)
            for s in range(2):
                sp.wait_ge(y_st[s], 16 * E * Q // 2)

        @block.gpsimd
        def _(pool):
            pool.memset(ident[:, :], 0.0).then_inc(ident0, 1)
            pool.wait_ge(ident0, 1)
            pool.affine_select(out=ident[:, :], in_=ident[:, :], compare_op=ALU.not_equal, fill=1.0,
                               base=0, pattern=[[-1, P]], channel_multiplier=1).then_inc(ident_made, 1)

            def indices(e, es):
                if at_least(e, 2):
                    for s in range(2):
                        pool.wait_ge(xg_ld[s], 16 * R * (Q // 2) * (e - 1))
                pool.tensor_copy(idx_e[es][:, :], gidx[:, bass.ds(e * CAP, CAP)]).then_inc(idx_done, 1)

            def gather(n, e, es, q):
                ready, used = count(pool, e + 1), count(pool, n - 1)
                pool.wait_ge(ident_made, 1)
                if q == 0:
                    pool.wait_ge(idx_done, ready)
                wait(pool, xt_done, used)
                for r in range(R):
                    pool.indirect_dma_start(
                        out=xg[q % 2][:, r, :], out_offset=None, in_=xn_rows,
                        in_offset=bass.IndirectOffsetOnAxis(ap=idx_e[es][:, q * R + r:q * R + r + 1], axis=0),
                    ).then_inc(xg_ld[q % 2], 16)

            indices(0, 0)
            gather(0, 0, 0, 0)
            gather(1, 0, 0, 1)

            def body(e, es, q):
                n = Q * e + q
                if q == 1 and below(e, E - 1):
                    indices(e + 1, 1 - es)
                if q < Q - 2:
                    gather(n + 2, e, es, q + 2)
                elif below(e, E - 1):
                    gather(n + 2, e + 1, 1 - es, q + 2 - Q)

            steps(pool, body)

        @block.tensor
        def _(pe):
            pe.wait_ge(ident_made, 1)

            def slots_T(n, q):
                pe.wait_ge(xg_ld[q % 2], 16 * R * rounds(n, q % 2))
                wait(pe, xlo_done, n)
                for r in range(R):
                    for c in range(DC):
                        last = pe.transpose(x_ps[:, c, r * P:(r + 1) * P], xg[q % 2][:, r, c * P:(c + 1) * P],
                                            ident[:, :])
                last.then_inc(xt_done, 1)

            def up(n, e, es, q, f):
                if f == 0:
                    pe.wait_ge(xlo_done, n + 1)
                    pe.wait_ge(xhi_done, n + 1)
                    if q == 0:
                        pe.wait_ge(wlo_done, 3 * (e + 1))
                wait(pe, hid_done, FC * n + f - 1)
                for k, bank in ((0, g_ps[f % 2]), (1, u_ps[f % 2])):
                    parts = [(w, x, c) for c in range(DC)
                             for w, x in ((whi, xhi), (whi, xlo), (wlo, xhi))]
                    for m, (w, x, c) in enumerate(parts):
                        last = pe.matmul(bank[:, :], w[k][es][:, c * F + f * P:c * F + (f + 1) * P],
                                         x[q % 2][:, c, :], start=m == 0, stop=m == len(parts) - 1)
                last.then_inc(gu_done, 1)

            def down(n, es, q):
                pe.wait_ge(hlo_done, FC * (n + 1))
                wait(pe, ya_done, n)
                wait(pe, yb_done, n)
                for r in range(R):
                    parts = [(h, w, f) for f in range(FC)
                             for h, w in ((hhi, whi), (hhi, wlo), (hlo, whi))]
                    for m, (h, w, f) in enumerate(parts):
                        last = pe.matmul(y_ps[:, r, :], h[q % 2][:, f, r * P:(r + 1) * P],
                                         w[2][es][:, f * D:(f + 1) * D], start=m == 0, stop=m == len(parts) - 1)
                last.then_inc(y_done, 1)

            slots_T(0, 0)

            def body(e, es, q):
                n = Q * e + q
                up(n, e, es, q, 0)
                up(n, e, es, q, 1)
                if q > 0:
                    down(n - 1, es, q - 1)
                elif at_least(e, 1):
                    down(n - 1, 1 - es, Q - 1)
                if below(e, E - 1) or q < Q - 1:
                    slots_T(n + 1, (q + 1) % Q)
                up(n, e, es, q, 2)
                up(n, e, es, q, 3)

            steps(pe, body)
            down(E * Q - 1, 1, Q - 1)

        @block.scalar
        def _(act):
            def slots_hi(n, q):
                act.wait_ge(xt_done, n + 1)
                wait(act, gu_done, FC * (n - 1))
                act.activation(xhi[q % 2][:, :, :], x_ps[:, :, :], ACT.Copy).then_inc(xhi_done, 1)

            def out_half(n, e, es, q):
                act.wait_ge(y_done, n + 1)
                if at_least(n, 2):
                    act.wait_ge(y_st[q % 2], 16 * (rounds(n, q % 2) - 1))
                act.wait_ge(we_done, e + 1)
                for r in range(R // 2):
                    last = act.activation(yo[q % 2][:, r, :], y_ps[:, r, :], ACT.Copy,
                                          scale=w_e[es][:, q * R + r:q * R + r + 1])
                last.then_inc(ya_done, 1)

            slots_hi(0, 0)

            def hidden(n, q, f):
                act.wait_ge(gu_done, FC * n + f + 1)
                wait(act, hid_done, FC * n + f - 1)
                act.activation(act_g[f % 2][:, :], g_ps[f % 2][:, :], ACT.Gelu).then_inc(gelu_done, 1)

            def hidden_hi(n, q, f):
                act.wait_ge(hid_done, FC * n + f + 1)
                if f == 0:
                    wait(act, y_done, n - 1)
                act.activation(hhi[q % 2][:, f, :], hid[f % 2][:, :], ACT.Copy).then_inc(hhi_done, 1)

            def body(e, es, q):
                n = Q * e + q
                hidden(n, q, 0)
                hidden_hi(n, q, 0)
                hidden(n, q, 1)
                hidden_hi(n, q, 1)
                if q > 0:
                    out_half(n - 1, e, es, q - 1)
                elif at_least(e, 1):
                    out_half(n - 1, e - 1, 1 - es, Q - 1)
                if below(e, E - 1) or q < Q - 1:
                    slots_hi(n + 1, (q + 1) % Q)
                hidden(n, q, 2)
                hidden_hi(n, q, 2)
                hidden(n, q, 3)
                hidden_hi(n, q, 3)

            steps(act, body)
            out_half(E * Q - 1, E - 1, 1, Q - 1)

        @block.vector
        def _(dve):
            def weight_parts(e, es, k):
                dve.wait_ge(w_ld[k], 16 * (e + 1))
                wait(dve, y_done, Q * (e - 1))
                dve.tensor_copy(whi[k][es][:, :], raw[k][:, :]).then_inc(whi_done, 1)
                dve.wait_ge(whi_done, 3 * e + k + 1)
                dve.tensor_tensor(wlo[k][es][:, :], raw[k][:, :], whi[k][es][:, :].bitcast(fp32),
                                  ALU.subtract).then_inc(wlo_done, 1)

            def shares(e, es):
                wait(dve, ya_done, Q * (e - 1))
                wait(dve, yb_done, Q * (e - 1))
                dve.tensor_copy(w_e[es][:, :], wts[:, bass.ds(e, 1), :]).then_inc(we_done, 1)

            def slots_lo(n, q):
                dve.wait_ge(xhi_done, n + 1)
                wait(dve, gu_done, FC * (n - 1))
                dve.tensor_tensor(xlo[q % 2][:, :, :], x_ps[:, :, :], xhi[q % 2][:, :, :].bitcast(fp32),
                                  ALU.subtract).then_inc(xlo_done, 1)

            def product(n, q, f):
                dve.wait_ge(gelu_done, FC * n + f + 1)
                wait(dve, hlo_done, FC * n + f - 1)
                dve.tensor_tensor(hid[f % 2][:, :], u_ps[f % 2][:, :], act_g[f % 2][:, :],
                                  ALU.mult).then_inc(hid_done, 1)

            def out_half(n, e, es, q):
                dve.wait_ge(ya_done, n + 1)
                dve.wait_ge(we_done, e + 1)
                for r in range(R // 2, R):
                    last = dve.tensor_scalar(yo[q % 2][:, r, :], y_ps[:, r, :], w_e[es][:, q * R + r:q * R + r + 1],
                                             None, ALU.mult)
                last.then_inc(yb_done, 1)

            def hidden_lo(n, q, f):
                dve.wait_ge(hhi_done, FC * n + f + 1)
                if f == 0:
                    wait(dve, y_done, n - 1)
                dve.tensor_tensor(hlo[q % 2][:, f, :], hid[f % 2][:, :], hhi[q % 2][:, f, :].bitcast(fp32),
                                  ALU.subtract).then_inc(hlo_done, 1)

            shares(0, 0)
            for k in range(3):
                weight_parts(0, 0, k)
            slots_lo(0, 0)

            def body(e, es, q):
                n = Q * e + q
                product(n, q, 0)
                hidden_lo(n, q, 0)
                product(n, q, 1)
                hidden_lo(n, q, 1)
                if q > 0:
                    out_half(n - 1, e, es, q - 1)
                elif at_least(e, 1):
                    out_half(n - 1, e - 1, 1 - es, Q - 1)
                if below(e, E - 1) or q < Q - 1:
                    slots_lo(n + 1, (q + 1) % Q)
                product(n, q, 2)
                hidden_lo(n, q, 2)
                product(n, q, 3)
                hidden_lo(n, q, 3)
                if below(e, E - 1):
                    if q == 0:
                        shares(e + 1, 1 - es)
                    else:
                        weight_parts(e + 1, 1 - es, q - 1)

            steps(dve, body)
            out_half(E * Q - 1, E - 1, 1, Q - 1)


def shared_phase(nc, sem, xn_d, x1_d, sg, su, sd, idx_col, eo_d, out):
    Q = 4
    N = Q * S
    STEPS = B // Q
    HALF = E * CAP // P
    with ExitStack() as ctx:
        def sb(name, shape, dt=fp32):
            return ctx.enter_context(nc.sbuf_tensor(name, shape, dt))

        def pb(name, shape):
            return ctx.enter_context(nc.psum_tensor(name, shape, fp32))

        ident = sb("s_ident", [P, P])
        tok_i = sb("s_tok_i", [P, S], u32)
        tok = sb("s_tok", [P, S])
        raw = [sb(f"s_raw{k}", [P, DC * F]) for k in range(3)]
        whi = [sb(f"s_whi{k}", [P, DC * F], f32r) for k in range(3)]
        wlo = [sb(f"s_wlo{k}", [P, DC * F], f32r) for k in range(3)]
        xg = [sb(f"s_x{s}", [P, Q, D]) for s in range(2)]
        res = [sb(f"s_res{s}", [P, Q, D]) for s in range(2)]
        eo = [sb(f"s_eo{s}", [P, HALF, Q, D]) for s in range(2)]
        ehi = sb("s_ehi", [P, HALF, Q, D], f32r)
        elo = sb("s_elo", [P, HALF, Q, D], f32r)
        hot = sb("s_hot", [P, HALF, Q, S], f32r)
        xhi = [sb(f"s_xhi{s}", [P, DC, N], f32r) for s in range(2)]
        xlo = [sb(f"s_xlo{s}", [P, DC, N], f32r) for s in range(2)]
        act_g = [sb(f"s_g{s}", [P, N]) for s in range(2)]
        hid = [sb(f"s_h{s}", [P, N]) for s in range(2)]
        hhi = [sb(f"s_hhi{s}", [P, FC, N], f32r) for s in range(2)]
        hlo = [sb(f"s_hlo{s}", [P, FC, N], f32r) for s in range(2)]
        yo = [sb(f"s_yo{s}", [P, Q, D]) for s in range(2)]
        x_ps = pb("s_x_ps", [P, DC, N])
        g_ps = [pb(f"s_g_ps{s}", [P, N]) for s in range(2)]
        u_ps = [pb(f"s_u_ps{s}", [P, N]) for s in range(2)]
        y_ps = pb("s_y_ps", [P, Q, D])

        ident0 = sem("s_ident0")
        ident_made = sem("s_ident_made")
        tok_made = sem("s_tok_made")
        tok_done = sem("s_tok_done")
        w_ld = [sem(f"s_w_ld{k}") for k in range(3)]
        whi_done = sem("s_whi_done")
        wlo_done = sem("s_wlo_done")
        x_ld = [sem(f"s_x_ld{s}") for s in range(2)]
        r_ld = [sem(f"s_r_ld{s}") for s in range(2)]
        eo_ld = [sem(f"s_eo_ld{s}") for s in range(2)]
        xt_done = sem("s_xt_done")
        xhi_done = sem("s_xhi_done")
        xlo_done = sem("s_xlo_done")
        hot_done = sem("s_hot_done")
        ehi_done = sem("s_ehi_done")
        elo_done = sem("s_elo_done")
        gu_done = sem("s_gu_done")
        gelu_done = sem("s_gelu_done")
        hid_done = sem("s_hid_done")
        hhi_done = sem("s_hhi_done")
        hlo_done = sem("s_hlo_done")
        y_done = sem("s_y_done")
        o_done = sem("s_o_done")
        o_st = [sem(f"s_o_st{s}") for s in range(2)]
        block = ctx.enter_context(nc.Block())

        def steps(eng, body):
            for n in range(4):
                body(n, n % 2)
            with eng.Fori(2, STEPS // 2 - 1) as i:
                for s in range(2):
                    body(2 * i + s, s)
            for n in range(STEPS - 2, STEPS):
                body(n, n % 2)

        def rounds(n, s):
            return n // 2 + 1 if isinstance(n, int) else (n - s) // 2 + 1

        eo_v = eo_d.rearrange("b (h e) r d -> (e r) h b d", h=HALF)

        @block.sync
        def _(sp):
            def load_tokens(n, s):
                wait(sp, xt_done, n - 1)
                sp.dma_start(xg[s][:, :, :], xn_d[bass.ds(n * Q, Q)].rearrange("b t d -> t b d")
                             ).then_inc(x_ld[s], 16)

            def load_routed(n, s):
                wait(sp, elo_done, n - 1)
                for half in range(HALF):
                    sp.dma_start(eo[s][:, half, :, :], eo_v[:, half, bass.ds(n * Q, Q), :]).then_inc(eo_ld[s], 16)

            def load_residual(n, s):
                wait(sp, o_done, n - 1)
                sp.dma_start(res[s][:, :, :], x1_d[bass.ds(n * Q, Q)].rearrange("b t d -> t b d")
                             ).then_inc(r_ld[s], 16)

            def store(n, s):
                sp.wait_ge(o_done, n + 1)
                sp.dma_start(out[bass.ds(n * Q, Q)].rearrange("b t d -> t b d"), yo[s][:, :, :]).then_inc(o_st[s], 16)

            load_tokens(0, 0)
            for k, w in enumerate((sg, su, sd)):
                sp.dma_start(raw[k][:, :].rearrange("p (c n) -> p c n", c=D // P if k < 2 else F // P),
                             w.rearrange("(c p) n -> p c n", p=P)).then_inc(w_ld[k], 16)
            load_tokens(1, 1)
            load_routed(0, 0)
            load_residual(0, 0)

            def body(n, s):
                if below(n, STEPS - 2):
                    load_tokens(n + 2, s)
                if below(n, STEPS - 1):
                    load_routed(n + 1, 1 - s)
                if at_least(n, 1):
                    store(n - 1, 1 - s)
                if below(n, STEPS - 1):
                    load_residual(n + 1, 1 - s)

            steps(sp, body)
            store(STEPS - 1, 1)
            for s in range(2):
                sp.wait_ge(o_st[s], 16 * STEPS // 2)

        @block.gpsimd
        def _(pool):
            pool.memset(ident[:, :], 0.0).then_inc(ident0, 1)
            pool.iota(tok_i[:, :], pattern=[[1, S]], base=0, channel_multiplier=0).then_inc(tok_made, 1)
            pool.wait_ge(ident0, 1)
            pool.affine_select(out=ident[:, :], in_=ident[:, :], compare_op=ALU.not_equal, fill=1.0,
                               base=0, pattern=[[-1, P]], channel_multiplier=1).then_inc(ident_made, 1)

            def body(n, s):
                pool.wait_ge(ehi_done, n + 1)
                wait(pool, y_done, n)
                pool.tensor_tensor(elo[:, :, :, :], eo[s][:, :, :, :], ehi[:, :, :, :].bitcast(fp32),
                                   ALU.subtract).then_inc(elo_done, 1)

            steps(pool, body)

        @block.tensor
        def _(pe):
            pe.wait_ge(ident_made, 1)

            def tokens_T(n, s):
                pe.wait_ge(x_ld[s], 16 * rounds(n, s))
                wait(pe, xlo_done, n)
                for r in range(Q):
                    for c in range(DC):
                        last = pe.transpose(x_ps[:, c, r * P:(r + 1) * P], xg[s][:, r, c * P:(c + 1) * P],
                                            ident[:, :])
                last.then_inc(xt_done, 1)

            def up(n, s, f):
                if f == 0:
                    pe.wait_ge(xlo_done, n + 1)
                    pe.wait_ge(xhi_done, n + 1)
                wait(pe, hid_done, FC * n + f - 1)
                for k, bank in ((0, g_ps[f % 2]), (1, u_ps[f % 2])):
                    parts = [(w, x, c) for c in range(DC)
                             for w, x in ((whi, xhi), (whi, xlo), (wlo, xhi))]
                    for m, (w, x, c) in enumerate(parts):
                        last = pe.matmul(bank[:, :], w[k][:, c * F + f * P:c * F + (f + 1) * P],
                                         x[s][:, c, :], start=m == 0, stop=m == len(parts) - 1)
                last.then_inc(gu_done, 1)

            def down(n, s):
                pe.wait_ge(hlo_done, FC * (n + 1))
                pe.wait_ge(elo_done, n + 1)
                pe.wait_ge(hot_done, n + 1)
                wait(pe, o_done, n)
                for r in range(Q):
                    parts = [(h, w, f) for f in range(FC)
                             for h, w in ((hhi, whi), (hhi, wlo), (hlo, whi))]
                    for m, (h, w, f) in enumerate(parts):
                        pe.matmul(y_ps[:, r, :], h[s][:, f, r * P:(r + 1) * P],
                                  w[2][:, f * D:(f + 1) * D], start=m == 0, stop=False)
                    for half in range(HALF):
                        for part in (ehi, elo):
                            last = pe.matmul(y_ps[:, r, :], hot[:, half, r, :], part[:, half, r, :],
                                             start=False, stop=half == HALF - 1 and part is elo)
                last.then_inc(y_done, 1)

            pe.wait_ge(wlo_done, 3)
            tokens_T(0, 0)

            def body(n, s):
                up(n, s, 0)
                up(n, s, 1)
                if at_least(n, 1):
                    down(n - 1, 1 - s)
                if below(n, STEPS - 1):
                    tokens_T(n + 1, 1 - s)
                up(n, s, 2)
                up(n, s, 3)

            steps(pe, body)
            down(STEPS - 1, 1)

        @block.scalar
        def _(act):
            def tokens_hi(n, s):
                act.wait_ge(xt_done, n + 1)
                wait(act, gu_done, FC * (n - 1))
                act.activation(xhi[s][:, :, :], x_ps[:, :, :], ACT.Copy).then_inc(xhi_done, 1)

            def hidden(n, s, f):
                act.wait_ge(gu_done, FC * n + f + 1)
                wait(act, hid_done, FC * n + f - 1)
                act.activation(act_g[f % 2][:, :], g_ps[f % 2][:, :], ACT.Gelu).then_inc(gelu_done, 1)

            def hidden_hi(n, s, f):
                act.wait_ge(hid_done, FC * n + f + 1)
                if f == 0:
                    wait(act, y_done, n - 1)
                act.activation(hhi[s][:, f, :], hid[f % 2][:, :], ACT.Copy).then_inc(hhi_done, 1)

            def routed_hi(n, s):
                act.wait_ge(eo_ld[s], 16 * HALF * rounds(n, s))
                wait(act, y_done, n)
                act.activation(ehi[:, :, :, :], eo[s][:, :, :, :], ACT.Copy).then_inc(ehi_done, 1)

            tokens_hi(0, 0)

            def body(n, s):
                hidden(n, s, 0)
                hidden_hi(n, s, 0)
                hidden(n, s, 1)
                hidden_hi(n, s, 1)
                if below(n, STEPS - 1):
                    tokens_hi(n + 1, 1 - s)
                routed_hi(n, s)
                hidden(n, s, 2)
                hidden_hi(n, s, 2)
                hidden(n, s, 3)
                hidden_hi(n, s, 3)

            steps(act, body)

        @block.vector
        def _(dve):
            for k in range(3):
                dve.wait_ge(w_ld[k], 16)
                dve.tensor_copy(whi[k][:, :], raw[k][:, :]).then_inc(whi_done, 1)
                dve.wait_ge(whi_done, k + 1)
                dve.tensor_tensor(wlo[k][:, :], raw[k][:, :], whi[k][:, :].bitcast(fp32),
                                  ALU.subtract).then_inc(wlo_done, 1)
            dve.wait_ge(tok_made, 1)
            dve.tensor_copy(tok[:, :], tok_i[:, :]).then_inc(tok_done, 1)
            dve.wait_ge(tok_done, 1)

            def tokens_lo(n, s):
                dve.wait_ge(xhi_done, n + 1)
                wait(dve, gu_done, FC * (n - 1))
                dve.tensor_tensor(xlo[s][:, :, :], x_ps[:, :, :], xhi[s][:, :, :].bitcast(fp32),
                                  ALU.subtract).then_inc(xlo_done, 1)

            def one_hot(n, s):
                wait(dve, y_done, n)
                for half in range(HALF):
                    last = dve.tensor_tensor(
                        hot[:, half, :, :], tok[:, :].rearrange("p (o t) -> p o t", o=1).to_broadcast([P, Q, S]),
                        idx_col[:, half, bass.ds(n * Q, Q)].rearrange("p (b o) -> p b o", o=1)
                        .to_broadcast([P, Q, S]), ALU.is_equal)
                last.then_inc(hot_done, 1)

            def product(n, s, f):
                dve.wait_ge(gelu_done, FC * n + f + 1)
                wait(dve, hlo_done, FC * n + f - 1)
                dve.tensor_tensor(hid[f % 2][:, :], u_ps[f % 2][:, :], act_g[f % 2][:, :],
                                  ALU.mult).then_inc(hid_done, 1)

            def finish(n, s):
                dve.wait_ge(y_done, n + 1)
                dve.wait_ge(r_ld[s], 16 * rounds(n, s))
                if at_least(n, 2):
                    dve.wait_ge(o_st[s], 16 * (rounds(n, s) - 1))
                dve.tensor_tensor(yo[s][:, :, :], y_ps[:, :, :], res[s][:, :, :], ALU.add).then_inc(o_done, 1)

            def hidden_lo(n, s, f):
                dve.wait_ge(hhi_done, FC * n + f + 1)
                if f == 0:
                    wait(dve, y_done, n - 1)
                dve.tensor_tensor(hlo[s][:, f, :], hid[f % 2][:, :], hhi[s][:, f, :].bitcast(fp32),
                                  ALU.subtract).then_inc(hlo_done, 1)

            tokens_lo(0, 0)

            def body(n, s):
                product(n, s, 0)
                hidden_lo(n, s, 0)
                product(n, s, 1)
                hidden_lo(n, s, 1)
                if at_least(n, 1):
                    finish(n - 1, 1 - s)
                if below(n, STEPS - 1):
                    tokens_lo(n + 1, 1 - s)
                product(n, s, 2)
                hidden_lo(n, s, 2)
                product(n, s, 3)
                hidden_lo(n, s, 3)
                one_hot(n, s)

            steps(dve, body)
            finish(STEPS - 1, 1)


def program(nc, x, ctx_in, wq, bq, wk, bk, wv, bv, rel, gate, wg, wu, wd, sg, su, sd, out):
    x1_d = nc.dram_tensor("x1_rows", [B, S, D], fp32).ap()
    xn_d = nc.dram_tensor("normed_rows", [B, S, D], fp32).ap()
    lg_d = nc.dram_tensor("router_logits", [B, S, E], fp32).ap()
    eo_d = nc.dram_tensor("expert_outputs", [B, E, CAP, D], fp32).ap()
    with ExitStack() as ctx:
        def sem(name):
            return ctx.enter_context(nc.semaphore(name))

        attention_phase(nc, sem, x, ctx_in, wq, wk, wv, bq, bk, bv, rel, gate, x1_d, xn_d, lg_d)
        gidx = ctx.enter_context(nc.sbuf_tensor("gidx", [P, E * CAP], u32))
        wts = ctx.enter_context(nc.sbuf_tensor("wts", [P, E, CAP], fp32))
        idx_col = ctx.enter_context(nc.sbuf_tensor("idx_col", [P, E * CAP // P, B], fp32))
        routing_phase(nc, sem, lg_d, gidx, wts, idx_col)
        expert_phase(nc, sem, xn_d.rearrange("b t d -> (b t) d"), wg, wu, wd, gidx, wts, eo_d)
        shared_phase(nc, sem, xn_d, x1_d, sg, su, sd, idx_col, eo_d, out)


_INS = ["x", "ctx_1024", "L0_xattn_Wq", "L0_xattn_bq", "L0_xattn_Wk", "L0_xattn_bk", "L0_xattn_Wv", "L0_xattn_bv",
        "L0_xattn_rel_emb", "L0_ffn_gate_w", "L0_ffn_Wg", "L0_ffn_Wu", "L0_ffn_Wd", "L0_ffn_Ws_g", "L0_ffn_Ws_u",
        "L0_ffn_Ws_d"]


def kernel(**inputs):
    import numpy as np
    import concourse.bacc as bacc
    from concourse.bass_utils import run_bass_kernel_spmd as run

    laid = {n: np.ascontiguousarray(inputs[n]) for n in _INS}
    for n in [_INS[1]] + _INS[9:]:
        laid[n] = np.ascontiguousarray(np.swapaxes(laid[n], -1, -2))
    rel = laid["L0_xattn_rel_emb"]
    n_rel = rel.shape[1]
    at = [j + n_rel if j < 0 else min(j, n_rel - 1) for j in range(MAXLEN - S, MAXLEN - S + RELS)]
    laid["L0_xattn_rel_emb"] = np.ascontiguousarray(rel[:, at[::-1]])
    nc = bacc.Bacc("TRN2", target_bir_lowering=False, num_devices=1)
    args = [nc.dram_tensor(f"in_{n}", laid[n].shape, mybir.dt.from_np(laid[n].dtype), kind="ExternalInput").ap()
            for n in _INS]
    out = nc.dram_tensor("out_0", (B, S, D), fp32, kind="ExternalOutput").ap()
    program(nc, *args, out)
    r = run(nc, [{f"in_{n}": laid[n] for n in _INS}], core_ids=[0])
    return r.results[0]["out_0"]
```

```python
import concourse.bass as bass
from concourse import mybir
from contextlib import ExitStack

B, S, D = 128, 128, 256
H = 16
DK = D // H
E = 16
F = 512
CAP = S * 2 // E
P = 128
DC = D // P
FC = F // P
G = 4
GH = H // G
VW = DK + 1
AVW = 64
SCALE = -float(DK) ** -0.5
EPS = 1e-5
LOWEST = -3.0e38
MAXLEN = 125
RELS = 2 * S - 1

fp32 = mybir.dt.float32
f32r = mybir.dt.float32r
u32 = mybir.dt.uint32
ALU = mybir.AluOpType
ACT = mybir.ActivationFunctionType
AX = mybir.AxisListType


def head_of(group, j):
    return GH * group + j


def wait(eng, sem, n):
    if not (isinstance(n, int) and n <= 0):
        eng.wait_ge(sem, n)


def count(eng, n):
    if not isinstance(n, int):
        eng.compute_val(n)
    return n


def batches(eng, body):
    for b in range(8):
        body(b, b % 4)
    with eng.Fori(2, B // 4 - 1) as i:
        for s in range(4):
            body(4 * i + s, s)
    for b in range(B - 4, B):
        body(b, b % 4)


def at_least(b, n):
    return not isinstance(b, int) or b >= n


def below(b, n):
    return not isinstance(b, int) or b < n


def attention_phase(nc, sem, x, ctx_in, wq, wk, wv, bq, bk, bv, rel, gate, x1_d, xn_d, xT_d, lg_d):
    with ExitStack() as ctx:
        def sb(name, shape, dt=fp32):
            return ctx.enter_context(nc.sbuf_tensor(name, shape, dt))

        def pb(name, shape):
            return ctx.enter_context(nc.psum_tensor(name, shape, fp32))

        ident = sb("a_ident", [P, P])
        flip = sb("flip", [P, P])
        wq_s = sb("wq_s", [P, DC, D])
        wk_s = sb("wk_s", [P, DC, D])
        wv_s = sb("wv_s", [P, DC, D])
        gate_s = sb("gate_s", [P, DC, E])
        bq_s = sb("bq_s", [P, DC])
        bk_s = sb("bk_s", [P, DC])
        bv_row = sb("bv_row", [1, D])
        bv_all = sb("bv_all", [P, D])
        bias_in = sb("bias_in", [P, H, S])
        nbias = sb("nbias", [P, G, GH, S])
        parity = sb("parity", [P, 2])
        bq_neg = sb("bq_neg", [P, DC])
        bk_par = sb("bk_par", [P, DC, 2])
        ppow = sb("ppow", [P, 1])
        epsc = sb("epsc", [P, 1])
        xt = [sb(f"xt{s}", [P, D]) for s in range(2)]
        ct = [sb(f"ct{s}", [P, DC, S]) for s in range(4)]
        xb = [sb(f"xb{s}", [P, D]) for s in range(4)]
        xn = [sb(f"xn{s}", [P, D]) for s in range(2)]
        st1 = [sb(f"st1{s}", [P, 6]) for s in range(2)]
        mv1 = [sb(f"mv1{s}", [P, 2]) for s in range(2)]
        rs1 = [sb(f"rs1{s}", [P, 2]) for s in range(2)]
        xT = [sb(f"xT{s}", [P, DC, P]) for s in range(2)]
        qk = [sb(f"qk{s}", [P, DC, 3, P]) for s in range(2)]
        qk_hi = [sb(f"qk_hi{s}", [P, DC, 3, P], f32r) for s in range(2)]
        qk_lo = [sb(f"qk_lo{s}", [P, DC, 3, P], f32r) for s in range(2)]
        v1 = [sb(f"v1{s}", [P, H * VW + AVW]) for s in range(2)]
        sc = [sb(f"sc{s}", [P, G, GH, S]) for s in range(2)]
        nmax = [sb(f"nmax{s}", [P, G, GH]) for s in range(2)]
        pr = [sb(f"pr{s}", [P, G, GH, S]) for s in range(2)]
        pT = [sb(f"pT{s}", [P, G, GH, S]) for s in range(2)]
        rinv = [sb(f"rinv{s}", [P, H]) for s in range(2)]
        att = [sb(f"att{s}", [P, D]) for s in range(2)]
        x1 = [sb(f"x1{s}", [P, D]) for s in range(2)]
        st2 = [sb(f"st2{s}", [P, 6]) for s in range(2)]
        mv2 = [sb(f"mv2{s}", [P, 2]) for s in range(2)]
        rs2 = [sb(f"rs2{s}", [P, 2]) for s in range(2)]
        x2 = [sb(f"x2{s}", [P, D]) for s in range(2)]
        x2T = [sb(f"x2T{s}", [P, DC, P]) for s in range(2)]
        lg = [sb(f"lg{s}", [P, E]) for s in range(2)]

        s_ps = [pb(f"s_ps{g}", [P, GH, S]) for g in range(G)]
        front = pb("front", [P, 4, P])
        ring = [pb(f"ring{k}", [P, 4, P]) for k in range(2)]
        v_ps = ring[0][:, 0:DC, :].rearrange("p a n -> p (a n)")
        o_ps = pb("o_ps", [P, H * VW + AVW + E])
        o_heads = o_ps[:, 0:H * VW].rearrange("p (h d) -> p h d", d=VW)
        o_logits = o_ps[:, H * VW + AVW:H * VW + AVW + E]

        N_CONST = 2 * DC * DC + 2 * G + 2
        const_ld = sem("const_ld")
        bv_ld = sem("bv_ld")
        rel_ld = sem("rel_ld")
        ident0 = sem("ident0")
        par0 = sem("par0")
        flip_made = sem("flip_made")
        flipped = sem("flipped")
        const_pool = sem("const_pool")
        const_dve = sem("const_dve")
        x_ld = [sem(f"x_ld{s}") for s in range(2)]
        c_ld = [sem(f"c_ld{s}") for s in range(4)]
        xb_done = sem("xb_done")
        stats1 = sem("stats1")
        var1 = sem("var1")
        eps1 = sem("eps1")
        rstd1 = sem("rstd1")
        xn_done = sem("xn_done")
        t_done = sem("t_done")
        xT_done = sem("xT_done")
        qk_done = sem("qk_done")
        v_done = sem("v_done")
        qkT_done = sem("qkT_done")
        qk_hi_done = sem("qk_hi_done")
        qk_lo_done = sem("qk_lo_done")
        v1_done = sem("v1_done")
        s_done = sem("s_done")
        max_done = sem("max_done")
        exp_done = sem("exp_done")
        pt_done = sem("pt_done")
        pT_done = sem("pT_done")
        av_done = sem("av_done")
        rinv_done = sem("rinv_done")
        att_done = sem("att_done")
        x1_done = sem("x1_done")
        stats2 = sem("stats2")
        var2 = sem("var2")
        eps2 = sem("eps2")
        rstd2 = sem("rstd2")
        x2_done = sem("x2_done")
        x2t_done = sem("x2t_done")
        x2T_done = sem("x2T_done")
        lgp_done = sem("lgp_done")
        lg_done = sem("lg_done")
        x1_st = [sem(f"x1_st{s}") for s in range(2)]
        x2_st = [sem(f"x2_st{s}") for s in range(2)]
        x2T_st = [sem(f"x2T_st{s}") for s in range(2)]
        lg_st = [sem(f"lg_st{s}") for s in range(2)]

        def rounds(b, s):
            return b // 2 + 1 if isinstance(b, int) else (b - s % 2) // 2 + 1

        def rounds_of_4(b, s):
            return b // 4 + 1 if isinstance(b, int) else (b - s % 4) // 4 + 1

        block = ctx.enter_context(nc.Block())

        @block.sync
        def _(sp):
            def load_x(b, s):
                wait(sp, xn_done, b - 1)
                wait(sp, xb_done, b - 1)
                sp.dma_start(xt[s % 2][:, :], x[b]).then_inc(x_ld[s % 2], 16)

            def load_ctx(b, s):
                wait(sp, v_done, b - 3)
                sp.dma_start(ct[s % 4][:, :, :], ctx_in[b].rearrange("(c p) t -> p c t", p=P)
                             ).then_inc(c_ld[s % 4], 16)

            load_x(0, 0)
            sp.dma_start(bv_row[:, :], bv.rearrange("(a n) -> a n", a=1)).then_inc(bv_ld, 16)
            load_ctx(0, 0)
            sp.dma_start(wv_s[:, :, :], wv.rearrange("(c p) n -> p c n", p=P)).then_inc(const_ld, 16)
            sp.dma_start(gate_s[:, :, :], gate.rearrange("(c p) n -> p c n", p=P)).then_inc(const_ld, 16)
            with nc.allow_non_contiguous_dma(reason="a bias vector is spread over the partitions once"):
                for dst, src in ((bq_s, bq), (bk_s, bk)):
                    for g in range(G):
                        sp.dma_start(dst[32 * g:32 * g + 32, :], src.rearrange("(g m r) -> g r m", g=G, m=DC)[g]
                                     ).then_inc(const_ld, 16)
            load_x(1, 1)
            win = bass.AP(rel.tensor, 0, [[1, P], [RELS, H], [1, S]])
            sp.dma_start(bias_in[:, :, :], win).then_inc(rel_ld, 16)
            load_ctx(1, 1)
            for b in range(2, 4):
                load_ctx(b, b)
                load_x(b, b)

            def store_rows(b, s):
                sp.wait_ge(x1_done, b + 1)
                sp.dma_start(x1_d[b], x1[s % 2][:, :]).then_inc(x1_st[s % 2], 16)
                sp.wait_ge(x2_done, b + 1)
                sp.dma_start(xn_d[b], x2[s % 2][:, :]).then_inc(x2_st[s % 2], 16)

            def store_rows_T(b, s):
                sp.wait_ge(x2T_done, b + 1)
                sp.dma_start(xT_d[:, b], x2T[s % 2][:, :, :]).then_inc(x2T_st[s % 2], 16)

            def store_logits(b, s):
                sp.wait_ge(lg_done, b + 1)
                sp.dma_start(lg_d[b], lg[s % 2][:, :]).then_inc(lg_st[s % 2], 16)

            def body(b, s):
                if below(b, B - 4):
                    load_x(b + 4, s)
                    load_ctx(b + 4, s)
                if at_least(b, 1):
                    store_rows(b - 1, s - 1)
                if at_least(b, 3):
                    store_rows_T(b - 3, s - 3)
                    store_logits(b - 3, s - 3)

            batches(sp, body)
            store_rows(B - 1, 3)
            for b in range(B - 3, B):
                store_rows_T(b, b % 4)
                store_logits(b, b % 4)
            for s in range(2):
                for done in (x1_st[s], x2_st[s], x2T_st[s], lg_st[s]):
                    sp.wait_ge(done, 16 * B // 2)

        @block.gpsimd
        def _(pool):
            pool.memset(ident[:, :], 0.0).then_inc(ident0, 1)
            pool.memset(flip[:, :], 0.0).then_inc(ident0, 1)
            pool.memset(parity[:, :], 0.0).then_inc(par0, 1)
            pool.memset(ppow[:, :], -0.5)
            pool.memset(epsc[:, :], EPS)
            pool.wait_ge(ident0, 2)
            pool.affine_select(out=flip[:, :], in_=flip[:, :], compare_op=ALU.not_equal, fill=-1.0,
                               base=1 - P, pattern=[[1, P]], channel_multiplier=1).then_inc(flip_made, 1)
            pool.affine_select(out=ident[:, :], in_=ident[:, :], compare_op=ALU.not_equal, fill=1.0,
                               base=0, pattern=[[-1, P]], channel_multiplier=1).then_inc(const_pool, 1)
            pool.wait_ge(bv_ld, 16)
            pool.partition_broadcast(bv_all[:, :], bv_row[0:1, :], channels=P).then_inc(const_pool, 1)
            pool.wait_ge(const_pool, 2)

            def keep_residual(b, s):
                pool.wait_ge(x_ld[s % 2], 16 * rounds(b, s))
                wait(pool, x1_done, b - 3)
                pool.tensor_tensor(xb[s % 4][:, :], xt[s % 2][:, :], bv_all[:, :], ALU.add).then_inc(xb_done, 1)

            def inverse_root(b, s, stats, mv, rs, eps, rstd):
                pool.wait_ge(stats, b + 1)
                pool.tensor_tensor(rs[s % 2][:, 1:2], mv[s % 2][:, 1:2], epsc[:, :], ALU.add).then_inc(eps, 1)
                pool.wait_ge(eps, b + 1)
                pool.tensor_tensor(rs[s % 2][:, 0:1], rs[s % 2][:, 1:2], ppow[:, :], ALU.pow).then_inc(rstd, 1)

            def qk_low(b, s):
                pool.wait_ge(qk_hi_done, b + 1)
                pool.tensor_tensor(qk_lo[s % 2][:, :, :, :], qk[s % 2][:, :, :, :],
                                   qk_hi[s % 2][:, :, :, :].bitcast(fp32), ALU.subtract).then_inc(qk_lo_done, 1)

            for b in range(3):
                keep_residual(b, b)
                inverse_root(b, b, stats1, mv1, rs1, eps1, rstd1)
            for b in range(2):
                qk_low(b, b)

            def residual(b, s):
                pool.wait_ge(att_done, b + 1)
                if at_least(b, 2):
                    pool.wait_ge(x1_st[s % 2], 16 * (rounds(b, s) - 1))
                pool.tensor_tensor(x1[s % 2][:, :], att[s % 2][:, :], xb[s % 4][:, :], ALU.add).then_inc(x1_done, 1)

            def second_norm(b, s):
                inverse_root(b, s, stats2, mv2, rs2, eps2, rstd2)
                ready, used, stored = count(pool, b + 1), count(pool, b - 1), count(pool, 16 * (rounds(b, s) - 1))
                pool.wait_ge(const_pool, 2)
                pool.wait_ge(rstd2, ready)
                wait(pool, x2t_done, used)
                wait(pool, x2_st[s % 2], stored)
                pool.tensor_scalar(x2[s % 2][:, :], x1[s % 2][:, :], mv2[s % 2][:, 0:1], rs2[s % 2][:, 0:1],
                                   ALU.subtract, ALU.mult).then_inc(x2_done, 1)

            def body(b, s):
                if at_least(b, 1):
                    residual(b - 1, s - 1)
                if below(b, B - 3):
                    keep_residual(b + 3, s + 3)
                    inverse_root(b + 3, s + 3, stats1, mv1, rs1, eps1, rstd1)
                if below(b, B - 2):
                    qk_low(b + 2, s + 2)
                if at_least(b, 1):
                    second_norm(b - 1, s - 1)

            batches(pool, body)
            residual(B - 1, 3)
            second_norm(B - 1, 3)

        @block.tensor
        def _(pe):
            pe.wait_ge(const_pool, 1)

            def mirror_bias():
                pe.wait_ge(rel_ld, 16)
                pe.wait_ge(flip_made, 1)
                for g in range(G):
                    for j in range(GH):
                        last = pe.matmul(s_ps[g][:, j, :], flip[:, :], bias_in[:, head_of(g, j), :],
                                         start=True, stop=True)
                last.then_inc(flipped, 1)

            def transposes(b, s):
                pe.wait_ge(xn_done, b + 1)
                wait(pe, x2T_done, b - 4)
                for c in range(DC):
                    last = pe.transpose(front[:, c, :], xn[s % 2][:, c * P:(c + 1) * P], ident[:, :])
                last.then_inc(t_done, 1)

            def project_qk(b, s):
                pe.wait_ge(c_ld[s % 4], 16 * rounds_of_4(b, s))
                pe.wait_ge(xT_done, b + 1)
                for w, src, o in ((wq_s, xT, 0), (wk_s, ct, DC)):
                    for m in range(DC):
                        for c in range(DC):
                            last = pe.matmul(front[:, o + m, :], w[:, c, m * P:(m + 1) * P],
                                             src[s % len(src)][:, c, :], start=c == 0, stop=c == DC - 1)
                last.then_inc(qk_done, 1)

            def project_v(b, s):
                wait(pe, pT_done, 4 * (b - 1) + 1)
                for c in range(DC):
                    last = pe.matmul(v_ps, ct[s % 4][:, c, :], wv_s[:, c, :], start=c == 0, stop=c == DC - 1)
                last.then_inc(v_done, 1)

            def rows_T(b, s):
                pe.wait_ge(x2_done, b + 1)
                pe.wait_ge(qkT_done, b + 5 if below(b, B - 4) else B)
                for c in range(DC):
                    last = pe.transpose(front[:, DC + c, :], x2[s % 2][:, c * P:(c + 1) * P], ident[:, :])
                last.then_inc(x2t_done, 1)

            def scores(b, s, pair):
                wait(pe, max_done, H * (b - 1) + 2 * GH * (pair + 1))
                if pair == 0:
                    if isinstance(b, int) and b == 0:
                        pe.wait_ge(const_dve, 7)
                    pe.wait_ge(qk_lo_done, b + 1)
                parts = ((qk_hi, qk_hi), (qk_hi, qk_lo), (qk_lo, qk_hi))
                for c in range(DC):
                    for m, (q, k) in enumerate(parts):
                        for g in (2 * pair, 2 * pair + 1):
                            rows = slice(32 * g, 32 * g + 32)
                            last = pe.matmul(s_ps[g][:, 2 * c:2 * c + 2, :], q[s % 2][rows, c, 0, :],
                                             k[s % 2][rows, c, 1:3, :], start=m == 0, stop=m == len(parts) - 1)
                last.then_inc(s_done, 1)

            def probs_T(b, s, g):
                pe.wait_ge(exp_done, H * b + GH * (g + 1))
                wait(pe, pT_done, 4 * b + g - 1)
                if g == 2:
                    pe.wait_ge(v1_done, b + 2 if below(b, B - 1) else B)
                for j in range(GH):
                    last = pe.transpose(ring[g % 2][:, j, :], pr[s % 2][:, g, j, :], ident[:, :])
                last.then_inc(pt_done, 1)

            def weigh_values(b, s, g):
                pe.wait_ge(pT_done, 4 * b + g + 1)
                if g == 0:
                    pe.wait_ge(v1_done, b + 1)
                    wait(pe, att_done, b)
                for j in range(GH):
                    at = head_of(g, j) * VW
                    last = pe.matmul(o_ps[:, at:at + AVW], pT[s % 2][:, g, j, :], v1[s % 2][:, at:at + AVW],
                                     start=True, stop=True)
                if g == G - 1:
                    last.then_inc(av_done, 1)

            def logits(b, s):
                pe.wait_ge(x2T_done, b + 1)
                for c in range(DC):
                    last = pe.matmul(o_logits, x2T[s % 2][:, c, :], gate_s[:, c, :], start=c == 0, stop=c == DC - 1)
                last.then_inc(lgp_done, 1)

            transposes(0, 0)
            pe.wait_ge(const_ld, 16 * N_CONST)
            project_qk(0, 0)
            project_v(0, 0)
            mirror_bias()
            pe.wait_ge(qkT_done, 1)
            transposes(1, 1)
            project_qk(1, 1)
            scores(0, 0, 0)
            scores(0, 0, 1)

            def body(b, s):
                if below(b, B - 1):
                    scores(b + 1, s + 1, 0)
                if at_least(b, 1):
                    weigh_values(b - 1, s - 1, 2)
                if below(b, B - 2):
                    pe.wait_ge(qkT_done, b + 2)
                    transposes(b + 2, s + 2)
                if at_least(b, 1):
                    weigh_values(b - 1, s - 1, 3)
                probs_T(b, s, 0)
                if below(b, B - 2):
                    project_qk(b + 2, s + 2)
                probs_T(b, s, 1)
                weigh_values(b, s, 0)
                if below(b, B - 1):
                    project_v(b + 1, s + 1)
                weigh_values(b, s, 1)
                if at_least(b, 2):
                    rows_T(b - 2, s - 2)
                if below(b, B - 1):
                    scores(b + 1, s + 1, 1)
                probs_T(b, s, 2)
                if at_least(b, 2):
                    logits(b - 2, s - 2)
                probs_T(b, s, 3)

            batches(pe, body)
            weigh_values(B - 1, 3, 2)
            weigh_values(B - 1, 3, 3)
            for b in range(B - 2, B):
                pe.wait_ge(x2T_done, b)
                rows_T(b, b % 4)
                pe.wait_ge(att_done, B)
                pe.wait_ge(lg_done, b)
                logits(b, b % 4)

        @block.scalar
        def _(act):
            for m in range(DC):
                for dst, src in ((wq_s, wq), (wk_s, wk)):
                    for c in range(DC):
                        act.dma_start(dst[:, c, m * P:(m + 1) * P].rearrange("p (g r) -> p g r", g=G),
                                     src[c * P:(c + 1) * P].rearrange("p (g m r) -> p m g r", g=G, m=DC)[:, m]
                                     ).then_inc(const_ld, 16)

            def front_T(b, s):
                act.wait_ge(t_done, b + 1)
                wait(act, qk_done, b - 1)
                act.activation(xT[s % 2][:, :, :], front[:, 0:DC, :], ACT.Copy).then_inc(xT_done, 1)

            def queries_and_keys(b, s):
                act.wait_ge(qk_done, b + 1)
                wait(act, qk_lo_done, b - 1)
                for c in range(DC):
                    act.activation(qk[s % 2][:, c, 0, :], front[:, c, :], ACT.Identity,
                                   bias=bq_neg[:, c:c + 1], scale=SCALE)
                    for j in range(2):
                        last = act.activation(qk[s % 2][:, c, 1 + j, :], front[:, DC + c, :], ACT.Identity,
                                              bias=bk_par[:, c, j:j + 1], scale=parity[:, j:j + 1])
                last.then_inc(qkT_done, 1)

            def values(b, s):
                act.wait_ge(v_done, b + 1)
                wait(act, av_done, b - 1)
                act.activation(v1[s % 2][:, 0:H * VW].rearrange("p (h d) -> p h d", d=VW)[:, :, 0:DK],
                               v_ps.rearrange("p (h d) -> p h d", d=DK),
                               ACT.Copy).then_inc(v1_done, 1)

            def rows(b, s):
                act.wait_ge(x2t_done, b + 1)
                wait(act, lgp_done, b - 1)
                if at_least(b, 2):
                    act.wait_ge(x2T_st[s % 2], 16 * (rounds(b, s) - 1))
                act.activation(x2T[s % 2][:, :, :], front[:, DC:2 * DC, :], ACT.Copy).then_inc(x2T_done, 1)

            def exps(b, s, g):
                wait(act, pt_done, 4 * (b - 2) + g + 1)
                for j in range(GH):
                    act.wait_ge(max_done, H * b + GH * g + j + 1)
                    act.activation(pr[s % 2][:, g, j, :], sc[s % 2][:, g, j, :], ACT.Exp,
                                   bias=nmax[s % 2][:, g, j:j + 1], scale=-1.0).then_inc(exp_done, 1)

            front_T(0, 0)
            act.wait_ge(const_dve, 6)
            queries_and_keys(0, 0)
            values(0, 0)
            front_T(1, 1)
            queries_and_keys(1, 1)

            def body(b, s):
                exps(b, s, 0)
                exps(b, s, 1)
                if below(b, B - 2):
                    front_T(b + 2, s + 2)
                exps(b, s, 2)
                if below(b, B - 2):
                    queries_and_keys(b + 2, s + 2)
                if below(b, B - 1):
                    values(b + 1, s + 1)
                exps(b, s, 3)
                if at_least(b, 2):
                    rows(b - 2, s - 2)

            batches(act, body)
            rows(B - 2, 2)
            rows(B - 1, 3)

        @block.vector
        def _(dve):
            for s in range(2):
                dve.memset(v1[s][:, H * VW:], 0.0)
                dve.memset(v1[s][:, 0:H * VW].rearrange("p (h d) -> p h d", d=VW)[:, :, DK:VW], 1.0
                           ).then_inc(const_dve, 1)

            def stats(src, b, s, st, mv, var, done):
                dve.bn_stats(st[s % 2][:, :], src[s % 2][:, :]).then_inc(var, 1)
                ready = count(dve, b + 1)
                dve.wait_ge(const_dve, 2)
                dve.wait_ge(var, ready)
                dve.bn_aggr(mv[s % 2][:, :], st[s % 2][:, :]).then_inc(done, 1)

            def stats_in(b, s):
                dve.wait_ge(x_ld[s % 2], 16 * rounds(b, s))
                wait(dve, rstd1, b - 1)
                stats(xt, b, s, st1, mv1, var1, stats1)

            def norm_in(b, s):
                dve.wait_ge(rstd1, b + 1)
                wait(dve, t_done, b - 1)
                dve.tensor_scalar(xn[s % 2][:, :], xt[s % 2][:, :], mv1[s % 2][:, 0:1], rs1[s % 2][:, 0:1],
                                  ALU.subtract, ALU.mult).then_inc(xn_done, 1)

            def add_bias_and_max(b, s, g):
                ready, used = count(dve, 2 * b + g // 2 + 1), count(dve, H * (b - 2) + GH * (g + 1))
                dve.wait_ge(const_dve, 7)
                dve.wait_ge(s_done, ready)
                wait(dve, exp_done, used)
                for j in range(GH):
                    dve.tensor_tensor_reduce(out=sc[s % 2][:, g, j, :], in0=s_ps[g][:, j, :], in1=nbias[:, g, j, :],
                                             scale=1.0, scalar=-LOWEST, op0=ALU.add, op1=ALU.min,
                                             accum_out=nmax[s % 2][:, g, j:j + 1]).then_inc(max_done, 1)

            def probs_out(b, s, g):
                dve.wait_ge(pt_done, 4 * b + g + 1)
                if g == 0:
                    wait(dve, av_done, b - 1)
                dve.tensor_copy(pT[s % 2][:, g, :, :], ring[g % 2][:, :, :]).then_inc(pT_done, 1)

            def normalise(b, s):
                dve.wait_ge(av_done, b + 1)
                wait(dve, x1_done, b - 1)
                dve.reciprocal(rinv[s % 2][:, :], o_heads[:, :, DK]).then_inc(rinv_done, 1)
                if at_least(b, 2):
                    logits_out(b - 2, s - 2)
                dve.wait_ge(rinv_done, b + 1)
                dve.tensor_tensor(att[s % 2][:, :].rearrange("p (h d) -> p h d", d=DK), o_heads[:, :, 0:DK],
                                  rinv[s % 2][:, :].rearrange("p (h o) -> p h o", o=1).to_broadcast([P, H, DK]),
                                  ALU.mult).then_inc(att_done, 1)

            def logits_out(b, s):
                dve.wait_ge(lgp_done, b + 1)
                if at_least(b, 2):
                    dve.wait_ge(lg_st[s % 2], 16 * (rounds(b, s) - 1))
                dve.tensor_copy(lg[s % 2][:, :], o_logits).then_inc(lg_done, 1)

            def stats_out(b, s):
                dve.wait_ge(x1_done, b + 1)
                wait(dve, x2_done, b - 1)
                stats(x1, b, s, st2, mv2, var2, stats2)

            def qk_high(b, s):
                dve.wait_ge(qkT_done, b + 1)
                wait(dve, s_done, 2 * (b - 1))
                dve.tensor_copy(qk_hi[s % 2][:, :, :, :], qk[s % 2][:, :, :, :]).then_inc(qk_hi_done, 1)

            for b in range(2):
                stats_in(b, b)
                norm_in(b, b)
            dve.wait_ge(const_pool, 2)
            dve.wait_ge(par0, 1)
            blocks = ident[:, :].rearrange("p (a j d) -> p j a d", j=2, d=DK)
            for j in range(2):
                dve.tensor_reduce(parity[:, j:j + 1], blocks[:, j, :, :], AX.XY, ALU.add).then_inc(const_dve, 1)
            dve.wait_ge(const_ld, 16 * N_CONST)
            dve.wait_ge(const_dve, 4)
            dve.tensor_scalar(bq_neg[:, :], bq_s[:, :], SCALE, None, ALU.mult).then_inc(const_dve, 1)
            for j in range(2):
                last = dve.tensor_scalar(bk_par[:, :, j], bk_s[:, :], parity[:, j:j + 1], None, ALU.mult)
            last.then_inc(const_dve, 1)
            qk_high(0, 0)
            dve.wait_ge(flipped, 1)
            for g in range(G):
                last = dve.tensor_copy(nbias[:, g, :, :], s_ps[g][:, :, :])
            last.then_inc(const_dve, 1)
            dve.wait_ge(const_dve, 7)
            stats_in(2, 2)
            norm_in(2, 2)
            qk_high(1, 1)
            add_bias_and_max(0, 0, 0)
            add_bias_and_max(0, 0, 1)

            def body(b, s):
                if at_least(b, 1):
                    probs_out(b - 1, s - 1, 2)
                    probs_out(b - 1, s - 1, 3)
                if below(b, B - 3):
                    stats_in(b + 3, s + 3)
                if at_least(b, 1):
                    normalise(b - 1, s - 1)
                probs_out(b, s, 0)
                add_bias_and_max(b, s, 2)
                probs_out(b, s, 1)
                add_bias_and_max(b, s, 3)
                if below(b, B - 2):
                    qk_high(b + 2, s + 2)
                if below(b, B - 1):
                    add_bias_and_max(b + 1, s + 1, 0)
                    add_bias_and_max(b + 1, s + 1, 1)
                if at_least(b, 1):
                    stats_out(b - 1, s - 1)
                if below(b, B - 3):
                    norm_in(b + 3, s + 3)

            batches(dve, body)
            probs_out(B - 1, 3, 2)
            probs_out(B - 1, 3, 3)
            normalise(B - 1, 3)
            stats_out(B - 1, 3)
            logits_out(B - 2, 2)
            logits_out(B - 1, 3)


def routing_phase(nc, sem, lg_d, gidx, wts, idx_col):
    HALF = E * CAP // P
    with ExitStack() as ctx:
        def sb(name, shape, dt=fp32):
            return ctx.enter_context(nc.sbuf_tensor(name, shape, dt))

        ident = sb("r_ident", [P, P])
        raw = sb("r_raw", [P, S, E])
        less = sb("r_less", [P, S, E])
        ex = sb("r_exp", [P, S, E])
        score = sb("r_score", [P, E, S])
        rest = sb("r_rest", [P, E, S])
        top = sb("r_max", [P, S])
        tot = sb("r_sum", [P, S])
        inv = sb("r_inv", [P, S])
        place = sb("r_place", [P, E, CAP], u32)
        place_f = sb("r_place_f", [P, E * CAP])
        first_row = sb("r_first_row", [P, 1], u32)
        first_row_f = sb("r_first_row_f", [P, 1])
        idx_ps = ctx.enter_context(nc.psum_tensor("r_idx_ps", [P, HALF, P], fp32))

        lg_ld = sem("r_lg_ld")
        zeroed = sem("r_zeroed")
        ident_made = sem("r_ident_made")
        rows_made = sem("r_rows_made")
        step = sem("r_step")
        exp_done = sem("r_exp_done")
        places = sem("r_places")
        turned = sem("r_turned")
        block = ctx.enter_context(nc.Block())

        @block.sync
        def _(sp):
            sp.dma_start(raw[:, :, :], lg_d[:, :, :]).then_inc(lg_ld, 16)

        @block.gpsimd
        def _(pool):
            pool.memset(ident[:, :], 0.0).then_inc(zeroed, 1)
            pool.iota(first_row[:, :], pattern=[[0, 1]], base=0, channel_multiplier=S).then_inc(rows_made, 1)
            pool.wait_ge(zeroed, 1)
            pool.affine_select(out=ident[:, :], in_=ident[:, :], compare_op=ALU.not_equal, fill=1.0,
                               base=0, pattern=[[-1, P]], channel_multiplier=1).then_inc(ident_made, 1)

        @block.scalar
        def _(act):
            act.wait_ge(step, 2)
            act.activation(ex[:, :, :], less[:, :, :], ACT.Exp).then_inc(exp_done, 1)

        @block.tensor
        def _(pe):
            pe.wait_ge(ident_made, 1)
            pe.wait_ge(places, 1)
            for half in range(HALF):
                last = pe.transpose(idx_ps[:, half, :], place_f[:, half * P:(half + 1) * P], ident[:, :])
            last.then_inc(turned, 1)

        @block.vector
        def _(dve):
            def per_token(t):
                return t[:, :].rearrange("p (t o) -> p t o", o=1).to_broadcast([P, S, E])

            dve.wait_ge(lg_ld, 16)
            dve.tensor_reduce(top[:, :], raw[:, :, :], AX.X, ALU.max).then_inc(step, 1)
            dve.wait_ge(step, 1)
            dve.tensor_tensor(less[:, :, :], raw[:, :, :], per_token(top), ALU.subtract).then_inc(step, 1)
            dve.wait_ge(exp_done, 1)
            dve.tensor_reduce(tot[:, :], ex[:, :, :], AX.X, ALU.add).then_inc(step, 1)
            dve.wait_ge(step, 3)
            dve.reciprocal(inv[:, :], tot[:, :]).then_inc(step, 1)
            dve.wait_ge(step, 4)
            dve.tensor_tensor(score[:, :, :].rearrange("p e t -> p t e"), ex[:, :, :], per_token(inv),
                              ALU.mult).then_inc(step, 1)
            dve.wait_ge(step, 5)
            for e in range(E):
                dve.max(wts[:, e, 0:8], score[:, e, :]).then_inc(step, 1)
            dve.wait_ge(step, 5 + E)
            for e in range(E):
                dve.max_index(place[:, e, 0:8], wts[:, e, 0:8], score[:, e, :]).then_inc(step, 1)
            for e in range(E):
                dve.match_replace(rest[:, e, :], wts[:, e, 0:8], score[:, e, :], -1.0).then_inc(step, 1)
            dve.wait_ge(step, 5 + 3 * E)
            for e in range(E):
                dve.max(wts[:, e, 8:16], rest[:, e, :]).then_inc(step, 1)
            dve.wait_ge(step, 5 + 4 * E)
            for e in range(E):
                dve.max_index(place[:, e, 8:16], wts[:, e, 8:16], rest[:, e, :]).then_inc(step, 1)
            dve.wait_ge(rows_made, 1)
            dve.wait_ge(step, 5 + 5 * E)
            dve.tensor_copy(place_f[:, :], place[:, :, :].rearrange("p e r -> p (e r)")).then_inc(places, 1)
            dve.tensor_copy(first_row_f[:, :], first_row[:, :]).then_inc(places, 1)
            dve.wait_ge(places, 2)
            dve.tensor_scalar(gidx[:, :], place_f[:, :], first_row_f[:, :], None, ALU.add)
            dve.wait_ge(turned, 1)
            dve.tensor_copy(idx_col[:, :, :], idx_ps[:, :, :])


def expert_phase(nc, sem, xn_rows, wg, wu, wd, shared_w, whi, wlo, gidx, wts, eo_d):
    Q = 4
    R = CAP // Q
    N = R * P
    with ExitStack() as ctx:
        def sb(name, shape, dt=fp32):
            return ctx.enter_context(nc.sbuf_tensor(name, shape, dt))

        def pb(name, shape):
            return ctx.enter_context(nc.psum_tensor(name, shape, fp32))

        ident = sb("e_ident", [P, P])
        raw = [sb(f"e_raw{k}", [P, DC * F]) for k in range(3)]
        idx_e = [sb(f"e_idx{s}", [P, CAP], u32) for s in range(2)]
        w_e = [sb(f"e_w{s}", [P, CAP]) for s in range(2)]
        xg = [sb(f"e_xg{s}", [P, R, D]) for s in range(2)]
        xhi = [sb(f"e_xhi{s}", [P, DC, N], f32r) for s in range(2)]
        xlo = [sb(f"e_xlo{s}", [P, DC, N], f32r) for s in range(2)]
        act_g = [sb(f"e_g{s}", [P, N]) for s in range(2)]
        hid = [sb(f"e_h{s}", [P, N]) for s in range(2)]
        hhi = [sb(f"e_hhi{s}", [P, FC, N], f32r) for s in range(2)]
        hlo = [sb(f"e_hlo{s}", [P, FC, N], f32r) for s in range(2)]
        yo = [sb(f"e_yo{s}", [P, R, D]) for s in range(2)]
        x_ps = pb("e_x_ps", [P, DC, N])
        g_ps = [pb(f"e_g_ps{s}", [P, N]) for s in range(2)]
        u_ps = [pb(f"e_u_ps{s}", [P, N]) for s in range(2)]
        y_ps = pb("e_y_ps", [P, R, D])

        ident0 = sem("e_ident0")
        ident_made = sem("e_ident_made")
        w_ld = [sem(f"e_w_ld{k}") for k in range(3)]
        whi_done = sem("e_whi_done")
        wlo_done = sem("e_wlo_done")
        idx_done = sem("e_idx_done")
        we_done = sem("e_we_done")
        xg_ld = [sem(f"e_xg_ld{s}") for s in range(2)]
        xt_done = sem("e_xt_done")
        xhi_done = sem("e_xhi_done")
        xlo_done = sem("e_xlo_done")
        gu_done = sem("e_gu_done")
        gelu_done = sem("e_gelu_done")
        hid_done = sem("e_hid_done")
        hhi_done = sem("e_hhi_done")
        hlo_done = sem("e_hlo_done")
        y_done = sem("e_y_done")
        ya_done = sem("e_ya_done")
        yb_done = sem("e_yb_done")
        y_st = [sem(f"e_y_st{s}") for s in range(2)]
        block = ctx.enter_context(nc.Block())

        w_src = [wg, wu, wd]

        def steps(eng, body):
            for e in range(2):
                for q in range(Q):
                    body(e, e % 2, q)
            with eng.Fori(1, E // 2 - 1) as i:
                for es in range(2):
                    for q in range(Q):
                        body(2 * i + es, es, q)
            for e in range(E - 2, E):
                for q in range(Q):
                    body(e, e % 2, q)

        def rounds(n, s):
            return n // 2 + 1 if isinstance(n, int) else (n - s) // 2 + 1

        @block.sync
        def _(sp):
            def load_weight(e, k):
                wait(sp, wlo_done, 3 * e + k - 2)
                src = shared_w[k] if isinstance(e, int) and e == E else w_src[k][e]
                sp.dma_start(raw[k][:, :].rearrange("p (c n) -> p c n", c=D // P if k < 2 else F // P),
                             src.rearrange("(c p) n -> p c n", p=P)).then_inc(w_ld[k], 16)

            for e in range(2):
                for k in range(3):
                    load_weight(e, k)

            def body(e, es, q):
                n = Q * e + q
                sp.wait_ge(ya_done, n + 1)
                sp.wait_ge(yb_done, n + 1)
                sp.dma_start(eo_d[:, e, q * R:(q + 1) * R, :], yo[q % 2][:, :, :]).then_inc(y_st[q % 2], 16)
                if q > 0 and below(e, E - 1):
                    load_weight(e + 2, q - 1)

            steps(sp, body)
            for s in range(2):
                sp.wait_ge(y_st[s], 16 * E * Q // 2)

        @block.gpsimd
        def _(pool):
            pool.memset(ident[:, :], 0.0).then_inc(ident0, 1)
            pool.wait_ge(ident0, 1)
            pool.affine_select(out=ident[:, :], in_=ident[:, :], compare_op=ALU.not_equal, fill=1.0,
                               base=0, pattern=[[-1, P]], channel_multiplier=1).then_inc(ident_made, 1)

            def indices(e, es):
                if at_least(e, 2):
                    for s in range(2):
                        pool.wait_ge(xg_ld[s], 16 * R * (Q // 2) * (e - 1))
                pool.tensor_copy(idx_e[es][:, :], gidx[:, bass.ds(e * CAP, CAP)]).then_inc(idx_done, 1)

            def gather(n, e, es, q):
                ready, used = count(pool, e + 1), count(pool, n - 1)
                pool.wait_ge(ident_made, 1)
                if q == 0:
                    pool.wait_ge(idx_done, ready)
                wait(pool, xt_done, used)
                for r in range(R):
                    pool.indirect_dma_start(
                        out=xg[q % 2][:, r, :], out_offset=None, in_=xn_rows,
                        in_offset=bass.IndirectOffsetOnAxis(ap=idx_e[es][:, q * R + r:q * R + r + 1], axis=0),
                    ).then_inc(xg_ld[q % 2], 16)

            indices(0, 0)
            gather(0, 0, 0, 0)
            gather(1, 0, 0, 1)

            def body(e, es, q):
                n = Q * e + q
                if q == 1 and below(e, E - 1):
                    indices(e + 1, 1 - es)
                if q < Q - 2:
                    gather(n + 2, e, es, q + 2)
                elif below(e, E - 1):
                    gather(n + 2, e + 1, 1 - es, q + 2 - Q)

            steps(pool, body)

        @block.tensor
        def _(pe):
            pe.wait_ge(ident_made, 1)

            def slots_T(n, q):
                pe.wait_ge(xg_ld[q % 2], 16 * R * rounds(n, q % 2))
                wait(pe, xlo_done, n)
                for r in range(R):
                    for c in range(DC):
                        last = pe.transpose(x_ps[:, c, r * P:(r + 1) * P], xg[q % 2][:, r, c * P:(c + 1) * P],
                                            ident[:, :])
                last.then_inc(xt_done, 1)

            def up(n, e, es, q, f):
                if f == 0:
                    pe.wait_ge(xlo_done, n + 1)
                    pe.wait_ge(xhi_done, n + 1)
                wait(pe, hid_done, FC * n + f - 1)
                for k, bank in ((0, g_ps[f % 2]), (1, u_ps[f % 2])):
                    if q == 0 and f == 0:
                        pe.wait_ge(wlo_done, 3 * e + k + 1)
                    parts = [(w, x, c) for c in range(DC)
                             for w, x in ((whi, xhi), (whi, xlo), (wlo, xhi))]
                    for m, (w, x, c) in enumerate(parts):
                        last = pe.matmul(bank[:, :], w[k][es][:, c * F + f * P:c * F + (f + 1) * P],
                                         x[q % 2][:, c, :], start=m == 0, stop=m == len(parts) - 1)
                last.then_inc(gu_done, 1)

            def down(n, e, es, q):
                pe.wait_ge(hlo_done, FC * (n + 1))
                if q == 0:
                    pe.wait_ge(wlo_done, 3 * e + 3)
                wait(pe, ya_done, n)
                wait(pe, yb_done, n)
                for r in range(R):
                    parts = [(h, w, f) for f in range(FC)
                             for h, w in ((hhi, whi), (hhi, wlo), (hlo, whi))]
                    for m, (h, w, f) in enumerate(parts):
                        last = pe.matmul(y_ps[:, r, :], h[q % 2][:, f, r * P:(r + 1) * P],
                                         w[2][es][:, f * D:(f + 1) * D], start=m == 0, stop=m == len(parts) - 1)
                last.then_inc(y_done, 1)

            slots_T(0, 0)

            def body(e, es, q):
                n = Q * e + q
                up(n, e, es, q, 0)
                up(n, e, es, q, 1)
                if q > 0:
                    down(n - 1, e, es, q - 1)
                elif at_least(e, 1):
                    down(n - 1, e - 1, 1 - es, Q - 1)
                if below(e, E - 1) or q < Q - 1:
                    slots_T(n + 1, (q + 1) % Q)
                up(n, e, es, q, 2)
                up(n, e, es, q, 3)

            steps(pe, body)
            down(E * Q - 1, E - 1, 1, Q - 1)

        @block.scalar
        def _(act):
            def slots_hi(n, q):
                act.wait_ge(xt_done, n + 1)
                wait(act, gu_done, FC * (n - 1))
                act.activation(xhi[q % 2][:, :, :], x_ps[:, :, :], ACT.Copy).then_inc(xhi_done, 1)

            def out_half(n, e, es, q):
                act.wait_ge(y_done, n + 1)
                if at_least(n, 2):
                    act.wait_ge(y_st[q % 2], 16 * (rounds(n, q % 2) - 1))
                act.wait_ge(we_done, e + 1)
                for r in range(R // 2):
                    last = act.activation(yo[q % 2][:, r, :], y_ps[:, r, :], ACT.Copy,
                                          scale=w_e[es][:, q * R + r:q * R + r + 1])
                last.then_inc(ya_done, 1)

            slots_hi(0, 0)

            def hidden(n, q, f):
                act.wait_ge(gu_done, FC * n + f + 1)
                wait(act, hid_done, FC * n + f - 1)
                act.activation(act_g[f % 2][:, :], g_ps[f % 2][:, :], ACT.Gelu).then_inc(gelu_done, 1)

            def hidden_hi(n, q, f):
                act.wait_ge(hid_done, FC * n + f + 1)
                if f == 0:
                    wait(act, y_done, n - 1)
                act.activation(hhi[q % 2][:, f, :], hid[f % 2][:, :], ACT.Copy).then_inc(hhi_done, 1)

            def body(e, es, q):
                n = Q * e + q
                hidden(n, q, 0)
                hidden_hi(n, q, 0)
                hidden(n, q, 1)
                hidden_hi(n, q, 1)
                if q > 0:
                    out_half(n - 1, e, es, q - 1)
                elif at_least(e, 1):
                    out_half(n - 1, e - 1, 1 - es, Q - 1)
                if below(e, E - 1) or q < Q - 1:
                    slots_hi(n + 1, (q + 1) % Q)
                hidden(n, q, 2)
                hidden_hi(n, q, 2)
                hidden(n, q, 3)
                hidden_hi(n, q, 3)

            steps(act, body)
            out_half(E * Q - 1, E - 1, 1, Q - 1)

        @block.vector
        def _(dve):
            def weight_parts(e, es, k):
                dve.wait_ge(w_ld[k], 16 * (e + 1))
                wait(dve, y_done, Q * (e - 1))
                dve.tensor_copy(whi[k][es][:, :], raw[k][:, :]).then_inc(whi_done, 1)
                dve.wait_ge(whi_done, 3 * e + k + 1)
                dve.tensor_tensor(wlo[k][es][:, :], raw[k][:, :], whi[k][es][:, :].bitcast(fp32),
                                  ALU.subtract).then_inc(wlo_done, 1)

            def shares(e, es):
                wait(dve, ya_done, Q * (e - 1))
                wait(dve, yb_done, Q * (e - 1))
                dve.tensor_copy(w_e[es][:, :], wts[:, bass.ds(e, 1), :]).then_inc(we_done, 1)

            def slots_lo(n, q):
                dve.wait_ge(xhi_done, n + 1)
                wait(dve, gu_done, FC * (n - 1))
                dve.tensor_tensor(xlo[q % 2][:, :, :], x_ps[:, :, :], xhi[q % 2][:, :, :].bitcast(fp32),
                                  ALU.subtract).then_inc(xlo_done, 1)

            def product(n, q, f):
                dve.wait_ge(gelu_done, FC * n + f + 1)
                wait(dve, hlo_done, FC * n + f - 1)
                dve.tensor_tensor(hid[f % 2][:, :], u_ps[f % 2][:, :], act_g[f % 2][:, :],
                                  ALU.mult).then_inc(hid_done, 1)

            def out_half(n, e, es, q):
                dve.wait_ge(ya_done, n + 1)
                dve.wait_ge(we_done, e + 1)
                for r in range(R // 2, R):
                    last = dve.tensor_scalar(yo[q % 2][:, r, :], y_ps[:, r, :], w_e[es][:, q * R + r:q * R + r + 1],
                                             None, ALU.mult)
                last.then_inc(yb_done, 1)

            def hidden_lo(n, q, f):
                dve.wait_ge(hhi_done, FC * n + f + 1)
                if f == 0:
                    wait(dve, y_done, n - 1)
                dve.tensor_tensor(hlo[q % 2][:, f, :], hid[f % 2][:, :], hhi[q % 2][:, f, :].bitcast(fp32),
                                  ALU.subtract).then_inc(hlo_done, 1)

            shares(0, 0)
            for k in range(3):
                weight_parts(0, 0, k)
            slots_lo(0, 0)

            def body(e, es, q):
                n = Q * e + q
                product(n, q, 0)
                hidden_lo(n, q, 0)
                product(n, q, 1)
                hidden_lo(n, q, 1)
                if q > 0:
                    out_half(n - 1, e, es, q - 1)
                elif at_least(e, 1):
                    out_half(n - 1, e - 1, 1 - es, Q - 1)
                if below(e, E - 1) or q < Q - 1:
                    slots_lo(n + 1, (q + 1) % Q)
                product(n, q, 2)
                hidden_lo(n, q, 2)
                product(n, q, 3)
                hidden_lo(n, q, 3)
                if q == 0 and below(e, E - 1):
                    shares(e + 1, 1 - es)
                elif q > 0:
                    weight_parts(e + 1, 1 - es, q - 1)

            steps(dve, body)
            out_half(E * Q - 1, E - 1, 1, Q - 1)


def shared_phase(nc, sem, xT_d, x1_d, whi, wlo, idx_col, eo_d, out):
    Q = 4
    N = Q * S
    STEPS = B // Q
    HALF = E * CAP // P
    with ExitStack() as ctx:
        def sb(name, shape, dt=fp32):
            return ctx.enter_context(nc.sbuf_tensor(name, shape, dt))

        def pb(name, shape):
            return ctx.enter_context(nc.psum_tensor(name, shape, fp32))

        tok_i = sb("s_tok_i", [P, S], u32)
        tok = sb("s_tok", [P, S])
        xt = [sb(f"s_xt{s}", [P, Q, DC, S]) for s in range(2)]
        res = [sb(f"s_res{s}", [P, Q, D]) for s in range(2)]
        eo = [sb(f"s_eo{s}", [P, HALF, Q, D]) for s in range(2)]
        ehi = sb("s_ehi", [P, HALF, Q, D], f32r)
        elo = sb("s_elo", [P, HALF, Q, D], f32r)
        hot = sb("s_hot", [P, HALF, Q, S], f32r)
        xhi = [sb(f"s_xhi{s}", [P, DC, N], f32r) for s in range(2)]
        xlo = [sb(f"s_xlo{s}", [P, DC, N], f32r) for s in range(2)]
        act_g = [sb(f"s_g{s}", [P, N]) for s in range(2)]
        hid = [sb(f"s_h{s}", [P, N]) for s in range(2)]
        hhi = [sb(f"s_hhi{s}", [P, FC, N], f32r) for s in range(2)]
        hlo = [sb(f"s_hlo{s}", [P, FC, N], f32r) for s in range(2)]
        yo = [sb(f"s_yo{s}", [P, Q, D]) for s in range(2)]
        g_ps = [pb(f"s_g_ps{s}", [P, N]) for s in range(2)]
        u_ps = [pb(f"s_u_ps{s}", [P, N]) for s in range(2)]
        y_ps = pb("s_y_ps", [P, Q, D])

        tok_made = sem("s_tok_made")
        tok_done = sem("s_tok_done")
        x_ld = [sem(f"s_x_ld{s}") for s in range(2)]
        r_ld = [sem(f"s_r_ld{s}") for s in range(2)]
        eo_ld = [sem(f"s_eo_ld{s}") for s in range(2)]
        xhi_done = sem("s_xhi_done")
        xlo_done = sem("s_xlo_done")
        hot_done = sem("s_hot_done")
        ehi_done = sem("s_ehi_done")
        elo_done = sem("s_elo_done")
        gu_done = sem("s_gu_done")
        gelu_done = sem("s_gelu_done")
        hid_done = sem("s_hid_done")
        hhi_done = sem("s_hhi_done")
        hlo_done = sem("s_hlo_done")
        y_done = sem("s_y_done")
        o_done = sem("s_o_done")
        o_st = [sem(f"s_o_st{s}") for s in range(2)]
        block = ctx.enter_context(nc.Block())

        def steps(eng, body):
            for n in range(4):
                body(n, n % 2)
            with eng.Fori(2, STEPS // 2 - 1) as i:
                for s in range(2):
                    body(2 * i + s, s)
            for n in range(STEPS - 2, STEPS):
                body(n, n % 2)

        def rounds(n, s):
            return n // 2 + 1 if isinstance(n, int) else (n - s) // 2 + 1

        eo_v = eo_d.rearrange("b (h e) r d -> (e r) h b d", h=HALF)

        @block.sync
        def _(sp):
            def load_tokens(n, s):
                wait(sp, xlo_done, n - 1)
                sp.dma_start(xt[s][:, :, :, :], xT_d[:, bass.ds(n * Q, Q)]).then_inc(x_ld[s], 16)

            def load_routed(n, s):
                wait(sp, elo_done, n - 1)
                for half in range(HALF):
                    sp.dma_start(eo[s][:, half, :, :], eo_v[:, half, bass.ds(n * Q, Q), :]).then_inc(eo_ld[s], 16)

            def load_residual(n, s):
                wait(sp, o_done, n - 1)
                sp.dma_start(res[s][:, :, :], x1_d[bass.ds(n * Q, Q)].rearrange("b t d -> t b d")
                             ).then_inc(r_ld[s], 16)

            def store(n, s):
                sp.wait_ge(o_done, n + 1)
                sp.dma_start(out[bass.ds(n * Q, Q)].rearrange("b t d -> t b d"), yo[s][:, :, :]).then_inc(o_st[s], 16)

            load_tokens(0, 0)
            load_tokens(1, 1)
            load_routed(0, 0)
            load_residual(0, 0)

            def body(n, s):
                if below(n, STEPS - 2):
                    load_tokens(n + 2, s)
                if below(n, STEPS - 1):
                    load_routed(n + 1, 1 - s)
                if at_least(n, 1):
                    store(n - 1, 1 - s)
                if below(n, STEPS - 1):
                    load_residual(n + 1, 1 - s)

            steps(sp, body)
            store(STEPS - 1, 1)
            for s in range(2):
                sp.wait_ge(o_st[s], 16 * STEPS // 2)

        @block.gpsimd
        def _(pool):
            pool.iota(tok_i[:, :], pattern=[[1, S]], base=0, channel_multiplier=0).then_inc(tok_made, 1)

            def body(n, s):
                pool.wait_ge(ehi_done, n + 1)
                wait(pool, y_done, n)
                pool.tensor_tensor(elo[:, :, :, :], eo[s][:, :, :, :], ehi[:, :, :, :].bitcast(fp32),
                                   ALU.subtract).then_inc(elo_done, 1)

            steps(pool, body)

        @block.tensor
        def _(pe):
            def up(n, s, f):
                if f == 0:
                    pe.wait_ge(xlo_done, n + 1)
                    pe.wait_ge(xhi_done, n + 1)
                wait(pe, hid_done, FC * n + f - 1)
                for k, bank in ((0, g_ps[f % 2]), (1, u_ps[f % 2])):
                    parts = [(w, x, c) for c in range(DC)
                             for w, x in ((whi, xhi), (whi, xlo), (wlo, xhi))]
                    for m, (w, x, c) in enumerate(parts):
                        last = pe.matmul(bank[:, :], w[k][0][:, c * F + f * P:c * F + (f + 1) * P],
                                         x[s][:, c, :], start=m == 0, stop=m == len(parts) - 1)
                last.then_inc(gu_done, 1)

            def down(n, s):
                pe.wait_ge(hlo_done, FC * (n + 1))
                pe.wait_ge(elo_done, n + 1)
                pe.wait_ge(hot_done, n + 1)
                wait(pe, o_done, n)
                for r in range(Q):
                    parts = [(h, w, f) for f in range(FC)
                             for h, w in ((hhi, whi), (hhi, wlo), (hlo, whi))]
                    for m, (h, w, f) in enumerate(parts):
                        pe.matmul(y_ps[:, r, :], h[s][:, f, r * P:(r + 1) * P],
                                  w[2][0][:, f * D:(f + 1) * D], start=m == 0, stop=False)
                    for half in range(HALF):
                        for part in (ehi, elo):
                            last = pe.matmul(y_ps[:, r, :], hot[:, half, r, :], part[:, half, r, :],
                                             start=False, stop=half == HALF - 1 and part is elo)
                last.then_inc(y_done, 1)

            def body(n, s):
                up(n, s, 0)
                up(n, s, 1)
                if at_least(n, 1):
                    down(n - 1, 1 - s)
                up(n, s, 2)
                up(n, s, 3)

            steps(pe, body)
            down(STEPS - 1, 1)

        @block.scalar
        def _(act):
            def tokens_hi(n, s):
                act.wait_ge(x_ld[s], 16 * rounds(n, s))
                wait(act, gu_done, FC * (n - 1))
                act.activation(xhi[s][:, :, :].rearrange("p c (b t) -> p c b t", t=S),
                               xt[s][:, :, :, :].rearrange("p b c t -> p c b t"), ACT.Copy).then_inc(xhi_done, 1)

            def hidden(n, s, f):
                act.wait_ge(gu_done, FC * n + f + 1)
                wait(act, hid_done, FC * n + f - 1)
                act.activation(act_g[f % 2][:, :], g_ps[f % 2][:, :], ACT.Gelu).then_inc(gelu_done, 1)

            def hidden_hi(n, s, f):
                act.wait_ge(hid_done, FC * n + f + 1)
                if f == 0:
                    wait(act, y_done, n - 1)
                act.activation(hhi[s][:, f, :], hid[f % 2][:, :], ACT.Copy).then_inc(hhi_done, 1)

            def routed_hi(n, s):
                act.wait_ge(eo_ld[s], 16 * HALF * rounds(n, s))
                wait(act, y_done, n)
                act.activation(ehi[:, :, :, :], eo[s][:, :, :, :], ACT.Copy).then_inc(ehi_done, 1)

            tokens_hi(0, 0)

            def body(n, s):
                hidden(n, s, 0)
                hidden_hi(n, s, 0)
                hidden(n, s, 1)
                hidden_hi(n, s, 1)
                if below(n, STEPS - 1):
                    tokens_hi(n + 1, 1 - s)
                routed_hi(n, s)
                hidden(n, s, 2)
                hidden_hi(n, s, 2)
                hidden(n, s, 3)
                hidden_hi(n, s, 3)

            steps(act, body)

        @block.vector
        def _(dve):
            dve.wait_ge(tok_made, 1)
            dve.tensor_copy(tok[:, :], tok_i[:, :]).then_inc(tok_done, 1)
            dve.wait_ge(tok_done, 1)

            def tokens_lo(n, s):
                dve.wait_ge(xhi_done, n + 1)
                wait(dve, gu_done, FC * (n - 1))
                dve.tensor_tensor(xlo[s][:, :, :].rearrange("p c (b t) -> p c b t", t=S),
                                  xt[s][:, :, :, :].rearrange("p b c t -> p c b t"),
                                  xhi[s][:, :, :].bitcast(fp32).rearrange("p c (b t) -> p c b t", t=S),
                                  ALU.subtract).then_inc(xlo_done, 1)

            def one_hot(n, s):
                wait(dve, y_done, n)
                for half in range(HALF):
                    last = dve.tensor_tensor(
                        hot[:, half, :, :], tok[:, :].rearrange("p (o t) -> p o t", o=1).to_broadcast([P, Q, S]),
                        idx_col[:, half, bass.ds(n * Q, Q)].rearrange("p (b o) -> p b o", o=1)
                        .to_broadcast([P, Q, S]), ALU.is_equal)
                last.then_inc(hot_done, 1)

            def product(n, s, f):
                dve.wait_ge(gelu_done, FC * n + f + 1)
                wait(dve, hlo_done, FC * n + f - 1)
                dve.tensor_tensor(hid[f % 2][:, :], u_ps[f % 2][:, :], act_g[f % 2][:, :],
                                  ALU.mult).then_inc(hid_done, 1)

            def finish(n, s):
                dve.wait_ge(y_done, n + 1)
                dve.wait_ge(r_ld[s], 16 * rounds(n, s))
                if at_least(n, 2):
                    dve.wait_ge(o_st[s], 16 * (rounds(n, s) - 1))
                dve.tensor_tensor(yo[s][:, :, :], y_ps[:, :, :], res[s][:, :, :], ALU.add).then_inc(o_done, 1)

            def hidden_lo(n, s, f):
                dve.wait_ge(hhi_done, FC * n + f + 1)
                if f == 0:
                    wait(dve, y_done, n - 1)
                dve.tensor_tensor(hlo[s][:, f, :], hid[f % 2][:, :], hhi[s][:, f, :].bitcast(fp32),
                                  ALU.subtract).then_inc(hlo_done, 1)

            tokens_lo(0, 0)

            def body(n, s):
                product(n, s, 0)
                hidden_lo(n, s, 0)
                product(n, s, 1)
                hidden_lo(n, s, 1)
                if at_least(n, 1):
                    finish(n - 1, 1 - s)
                if below(n, STEPS - 1):
                    tokens_lo(n + 1, 1 - s)
                product(n, s, 2)
                hidden_lo(n, s, 2)
                product(n, s, 3)
                hidden_lo(n, s, 3)
                one_hot(n, s)

            steps(dve, body)
            finish(STEPS - 1, 1)


def program(nc, x, ctx_in, wq, bq, wk, bk, wv, bv, rel, gate, wg, wu, wd, sg, su, sd, out):
    x1_d = nc.dram_tensor("x1_rows", [B, S, D], fp32).ap()
    xn_d = nc.dram_tensor("normed_rows", [B, S, D], fp32).ap()
    xT_d = nc.dram_tensor("normed_rows_transposed", [P, B, DC, S], fp32).ap()
    lg_d = nc.dram_tensor("router_logits", [B, S, E], fp32).ap()
    eo_d = nc.dram_tensor("expert_outputs", [B, E, CAP, D], fp32).ap()
    with ExitStack() as ctx:
        def sem(name):
            return ctx.enter_context(nc.semaphore(name))

        attention_phase(nc, sem, x, ctx_in, wq, wk, wv, bq, bk, bv, rel, gate, x1_d, xn_d, xT_d, lg_d)
        gidx = ctx.enter_context(nc.sbuf_tensor("gidx", [P, E * CAP], u32))
        wts = ctx.enter_context(nc.sbuf_tensor("wts", [P, E, CAP], fp32))
        idx_col = ctx.enter_context(nc.sbuf_tensor("idx_col", [P, E * CAP // P, B], fp32))
        routing_phase(nc, sem, lg_d, gidx, wts, idx_col)
        whi = [[ctx.enter_context(nc.sbuf_tensor(f"whi{k}{s}", [P, DC * F], f32r)) for s in range(2)] for k in range(3)]
        wlo = [[ctx.enter_context(nc.sbuf_tensor(f"wlo{k}{s}", [P, DC * F], f32r)) for s in range(2)] for k in range(3)]
        expert_phase(nc, sem, xn_d.rearrange("b t d -> (b t) d"), wg, wu, wd, (sg, su, sd), whi, wlo, gidx, wts, eo_d)
        shared_phase(nc, sem, xT_d, x1_d, whi, wlo, idx_col, eo_d, out)


_INS = ["x", "ctx_1024", "L0_xattn_Wq", "L0_xattn_bq", "L0_xattn_Wk", "L0_xattn_bk", "L0_xattn_Wv", "L0_xattn_bv",
        "L0_xattn_rel_emb", "L0_ffn_gate_w", "L0_ffn_Wg", "L0_ffn_Wu", "L0_ffn_Wd", "L0_ffn_Ws_g", "L0_ffn_Ws_u",
        "L0_ffn_Ws_d"]


def kernel(**inputs):
    import numpy as np
    import concourse.bacc as bacc
    from concourse.bass_utils import run_bass_kernel_spmd as run

    laid = {n: np.ascontiguousarray(inputs[n]) for n in _INS}
    for n in [_INS[1]] + _INS[9:]:
        laid[n] = np.ascontiguousarray(np.swapaxes(laid[n], -1, -2))
    rel = laid["L0_xattn_rel_emb"]
    n_rel = rel.shape[1]
    at = [j + n_rel if j < 0 else min(j, n_rel - 1) for j in range(MAXLEN - S, MAXLEN - S + RELS)]
    laid["L0_xattn_rel_emb"] = np.ascontiguousarray(rel[:, at[::-1]])
    nc = bacc.Bacc("TRN2", target_bir_lowering=False, num_devices=1)
    args = [nc.dram_tensor(f"in_{n}", laid[n].shape, mybir.dt.from_np(laid[n].dtype), kind="ExternalInput").ap()
            for n in _INS]
    out = nc.dram_tensor("out_0", (B, S, D), fp32, kind="ExternalOutput").ap()
    program(nc, *args, out)
    r = run(nc, [{f"in_{n}": laid[n] for n in _INS}], core_ids=[0])
    return r.results[0]["out_0"]
```
